# Optimizing a Trainium2 kernel written in Bass

```python
import numpy as np
import jax
import jax.numpy as jnp

def _softmax(x, axis=-1):
    return jax.nn.softmax(x, axis=axis)

def _gelu(x):
    return jax.nn.gelu(x, approximate=True)

def _silu(x):
    return jax.nn.silu(x)

def _sigmoid(x):
    return jax.nn.sigmoid(x)

def _layernorm(x, axis=-1, eps=1e-05):
    m = jnp.mean(x, axis=axis, keepdims=True)
    v = jnp.var(x, axis=axis, keepdims=True)
    return (x - m) / jnp.sqrt(v + eps)

def _scatter_add(tgt, idx, src, axis=0):
    return tgt.at[idx].add(src)

def _segment_sum(src, seg, n):
    return jax.ops.segment_sum(src, seg, n)
kernel_name = 'mk_flamingo_gated_d1_seqx_r2_99710b'

def setup_inputs(seed: int=0):
    np.random.seed(seed)
    _w = jnp.asarray

    def _rec_inputs():
        import jax
        import jax.numpy as jnp
        _rk = jax.random.key(seed)
        x = -0.000125 + 0.9999 * jax.random.normal(jax.random.fold_in(_rk, 1), (4, 2048, 512), jnp.float32)
        _lenS = 2048 - jax.random.randint(jax.random.fold_in(_rk, 7), (4,), 0, max(1, 2048 // 4) + 1, jnp.int32)
        _lenS2 = 77 - jax.random.randint(jax.random.fold_in(_rk, 8), (4,), 0, max(1, 77 // 4) + 1, jnp.int32)
        _ctx_1024P = jax.random.normal(jax.random.fold_in(_rk, 11), (4, 16, 512), jnp.float32)
        _ctx_1024c = jax.random.dirichlet(jax.random.fold_in(_rk, 511), 0.3 * jnp.ones((16,), jnp.float32), (4, 77))
        _ctx_1024t = jnp.einsum('bsk,bkd->bsd', _ctx_1024c, _ctx_1024P)
        _ctx_1024t = _ctx_1024t * jax.lax.rsqrt(jnp.mean(jnp.square(_ctx_1024t)) + 1e-12) * 0.953939
        ctx_1024 = 4.13588e-05 + 0.999923 * (_ctx_1024t + 0.3 * jax.random.normal(jax.random.fold_in(_rk, 611), (4, 77, 512), jnp.float32))
        _g = jax.random.normal(jax.random.fold_in(_rk, 9001), (2, 1), jnp.float32)
        _g = jnp.sign(_g) * jnp.maximum(jnp.abs(_g), 1.0) + (_g == 0) * 1.0
        g_xattn = _g[0]
        g_ffn = _g[1]
        return (x, ctx_1024, g_xattn, g_ffn)
    x, ctx_1024, g_xattn, g_ffn = _rec_inputs()

    def _L0_xattn_setup():
        import jax, jax.numpy as jnp
        import numpy as np
        key = jax.random.key(seed)
        k1, k2 = jax.random.split(key)
        hidden_states = jax.random.normal(k1, (8, 2048, 512), dtype=jnp.float32)
        visual_hidden_state = jax.random.normal(k2, (8, 512, 512), dtype=jnp.float32)
        return {'hidden_states': hidden_states, 'visual_hidden_state': visual_hidden_state}
    _L0_xattn_all = _L0_xattn_setup()
    _L0_xattn_in = {k: v for k, v in _L0_xattn_all.items() if k in ()}
    del _L0_xattn_all

    def _L0_ffn_setup():
        import jax, jax.numpy as jnp
        import numpy as np
        ALPHA = 1.0
        key = jax.random.key(seed)
        ks = jax.random.split(key, 7)
        B, S, IN, OUT = (8, 4096, 512, 512)
        RANK, DDIM, UDIM = (4, 100, 50)
        return {'hidden_states': jax.random.normal(ks[0], (B, S, IN), dtype=jnp.float32), 'W': jax.random.normal(ks[1], (OUT, IN), dtype=jnp.float32) * 0.02, 'b': jax.random.normal(ks[2], (OUT,), dtype=jnp.float32) * 0.02, 'lora_down': jax.random.normal(ks[3], (RANK, DDIM), dtype=jnp.float32) * 0.1, 'lora_up': jax.random.normal(ks[4], (UDIM, RANK), dtype=jnp.float32) * 0.1, 'down_aux': jax.random.normal(ks[5], (DDIM, IN), dtype=jnp.float32) * 0.03, 'up_aux': jax.random.normal(ks[6], (OUT, UDIM), dtype=jnp.float32) * 0.03}
    _L0_ffn_all = _L0_ffn_setup()
    _L0_ffn_in = {k: v for k, v in _L0_ffn_all.items() if k in ('W', 'b', 'lora_down', 'lora_up', 'down_aux', 'up_aux')}
    del _L0_ffn_all
    return {'x': x, 'ctx_1024': ctx_1024, 'g_xattn': g_xattn, 'g_ffn': g_ffn, 'L0_ffn_W': _L0_ffn_in['W'], 'L0_ffn_b': _L0_ffn_in['b'], 'L0_ffn_lora_down': _L0_ffn_in['lora_down'], 'L0_ffn_lora_up': _L0_ffn_in['lora_up'], 'L0_ffn_down_aux': _L0_ffn_in['down_aux'], 'L0_ffn_up_aux': _L0_ffn_in['up_aux']}

def reference(x, ctx_1024, g_xattn, g_ffn, L0_ffn_W, L0_ffn_b, L0_ffn_lora_down, L0_ffn_lora_up, L0_ffn_down_aux, L0_ffn_up_aux):
    import jax
    import jax.numpy as jnp

    def _L0_xattn_ref(hidden_states, visual_hidden_state):
        import jax, jax.numpy as jnp
        import numpy as np
        fusion_scores = jnp.einsum('bsd,bvd->bsv', hidden_states, visual_hidden_state)
        fusion_probs = jax.nn.softmax(fusion_scores, axis=-1)
        fusion_output = jnp.einsum('bsv,bvd->bsd', fusion_probs, visual_hidden_state)
        return fusion_output

    def _L0_ffn_ref(hidden_states, W, b, lora_down, lora_up, down_aux, up_aux):
        import jax, jax.numpy as jnp
        import numpy as np
        ALPHA = 1.0
        lilora_weight = up_aux @ (lora_up @ (lora_down @ down_aux))
        base = jnp.einsum('bsi,oi->bso', hidden_states, W) + b
        delta = jnp.einsum('bsi,oi->bso', hidden_states, lilora_weight)
        return base + ALPHA * delta
    x = x + jnp.tanh(g_xattn[0]) * _L0_xattn_ref(_layernorm(x, axis=-1), ctx_1024)
    x = x + jnp.tanh(g_ffn[0]) * _L0_ffn_ref(_layernorm(x, axis=-1), L0_ffn_W, L0_ffn_b, L0_ffn_lora_down, L0_ffn_lora_up, L0_ffn_down_aux, L0_ffn_up_aux)
    return x

_drawn_inputs = setup_inputs


def setup_inputs(seed=0):
    import zlib

    import numpy as np

    out = dict(_drawn_inputs(seed))
    spreads = {}
    factors = {'L0_ffn_b': 4.324,
     'L0_ffn_lora_down': 3.111,
     'L0_ffn_lora_up': 3.38,
     'L0_ffn_down_aux': 3.202,
     'L0_ffn_up_aux': 3.347}
    for name, (base, spread) in spreads.items():
        noise = np.random.default_rng([zlib.crc32(name.encode()), seed]).standard_normal(out[name].shape)
        drawn = base * np.exp(spread * noise) if base else spread * noise
        out[name] = jnp.asarray(drawn.astype(out[name].dtype))
    for name, factor in factors.items():
        out[name] = (out[name] * factor).astype(out[name].dtype)
    return out
```

```python
from contextlib import ExitStack

import concourse.bass as bass
from concourse import mybir

F32 = mybir.dt.float32
F32R = mybir.dt.float32r
ALU = mybir.AluOpType
ACT = mybir.ActivationFunctionType
AX = mybir.AxisListType

P = 128
EPS = 1e-5
XRING = 8
UNIT = 2
ORING = 4


def build_kernel(nc, x, ctx_in, g_xattn, g_ffn, W, b, ld_t, lu_t, down, up_t, out):
    B, S, D = x.shape
    V = ctx_in.shape[1]
    R_, DD = ld_t.shape[1], ld_t.shape[0]
    U = lu_t.shape[1]
    KC = D // P
    TB = S // P
    T = B * TB
    HB = XRING
    PREP = HB + 2
    H = D // 2
    VP = V + 1
    CUT = (3 * V + 1) // 2 - V
    K2 = V + CUT
    assert TB == 2 * HB and 2 * K2 == 3 * V + 1 and K2 <= P and D == 512

    x_units = x.rearrange("b (u p n) d -> (b u) p n d", p=P, n=UNIT)
    out_units = out.rearrange("b (u p n) d -> (b u) p n d", p=P, n=UNIT)

    with ExitStack() as stack:
        def sb(name, shape, dt=F32):
            return stack.enter_context(nc.sbuf_tensor(name, shape, dt))

        def ps(name, shape, dt=F32):
            return stack.enter_context(nc.psum_tensor(name, shape, dt))

        def sem(name):
            return stack.enter_context(nc.semaphore(name))

        ident = sb("ident", [P, P])
        gates = sb("gates", [P, 2])
        tg = sb("tg", [P, 2])
        half_neg = sb("half_neg", [P, 1])
        eps = sb("eps", [P, 1])
        bias = sb("bias", [P, D])
        bias_g = sb("bias_g", [P, D])
        ldt_sb = sb("ldt_sb", [DD, R_])
        lut_sb = sb("lut_sb", [R_, U])
        down_sb = sb("down_sb", [DD, D])
        upt_sb = sb("upt_sb", [U, D])
        l1_sb = sb("l1_sb", [R_, D])
        l2_sb = sb("l2_sb", [U, D])
        w_rows = sb("w_rows", [P, KC, D])
        w_sum = sb("w_sum", [P, KC, D])
        w_cent = sb("w_cent", [P, KC, D])
        w_bn = sb("w_bn", [P, KC, 6])
        w_mv = sb("w_mv", [P, KC, 2])
        wc = sb("wc", [P, KC, 2, D + VP], F32R)
        c_rows = sb("c_rows", [V, D])
        c_bn = sb("c_bn", [V, 6])
        c_mv = sb("c_mv", [V, 2])
        c_cent = sb("c_cent", [V, D])
        ct = sb("ct", [P, 2, KC, V], F32R)
        v_hi = sb("v_hi", [V, 2 * D], F32R)
        v_lo = sb("v_lo", [V, 2 * D], F32R)
        stacks = sb("stacks", [K2, 2, 2 * D], F32R)
        x_sb = sb("x_sb", [P, XRING, D])
        xT = sb("xT", [P, 2, 2, KC, P], F32R)
        bn = sb("bn", [P, 2, 6])
        mv = sb("mv", [P, 4, 2])
        var_eps = sb("var_eps", [P, 4])
        rstd = sb("rstd", [P, 4])
        s_max = sb("s_max", [P, 2])
        neg_max = sb("neg_max", [P, 2])
        expd = sb("expd", [P, 2, V])
        e_sum = sb("e_sum", [P, 2])
        e_inv = sb("e_inv", [P, 2])
        p_ext = sb("p_ext", [P, 4 * V])
        pT = sb("pT", [K2, 2, P], F32R)
        x1 = sb("x1", [P, 2, D])
        x1_sum = sb("x1_sum", [P, 2])
        x1_nmean = sb("x1_nmean", [P, 2])
        squares = sb("squares", [P, D])
        x1_var = sb("x1_var", [P, 4])
        var1_eps = sb("var1_eps", [P, 4])
        rstd1 = sb("rstd1", [P, 4])
        y_sb = sb("y_sb", [P, 2, D])
        x1_bias = sb("x1_bias", [P, 2, D])
        o_sb = sb("o_sb", [P, ORING, D])

        y_ps = ps("y_ps", [P, 2, 2, D])
        a_ps = ps("a_ps", [P, D])
        xt_ps = ps("xt_ps", [P, 2, KC, P])
        c_ps = ps("c_ps", [P, D])
        ct_ps = c_ps[:, 0:KC * V].rearrange("p (c v) -> p c v", c=KC)

        def scores(j):
            return y_ps[:, j, 1, H:H + V]

        def p_transposed(j):
            return y_ps[0:K2, j, 0, H:D].rearrange("p (s r) -> p s r", s=2)

        def w_bank(c):
            return y_ps[:, c // 2, c % 2, :]

        ld_x = [sem(f"ld_x{i}") for i in range(XRING // UNIT)]
        st_o = [sem(f"st_o{i}") for i in range(ORING // UNIT)]
        ld_gate, ld_bias, ld_low, ld_w, ld_ctx = (sem(n) for n in ("ld_gate", "ld_bias", "ld_low", "ld_w", "ld_ctx"))
        zeroed, ident_ok, tg_ok, biasg_ok = (sem(n) for n in ("zeroed", "ident_ok", "tg_ok", "biasg_ok"))
        low_mm, low_sb = sem("low_mm"), sem("low_sb")
        w_own, w_centred, w_tr, w_hi_ok, w_lo_ok = (sem(n) for n in ("w_own", "w_centred", "w_tr", "w_hi_ok", "w_lo_ok"))
        c_own, c_centred, c_tr, ct_hi_ok, ct_lo_ok = (sem(n) for n in ("c_own", "c_centred", "c_tr", "ct_hi_ok", "ct_lo_ok"))
        c_cols, cw_mm, v_hi_ok, v_lo_ok, stacked = (sem(n) for n in ("c_cols", "cw_mm", "v_hi_ok", "v_lo_ok", "stacked"))
        xt_ready, xh_ready, xl_ready, x_done = (sem(n) for n in ("xt_ready", "xh_ready", "xl_ready", "x_done"))
        bn_ok, mv_ready, rs_own, rstd_ready = (sem(n) for n in ("bn_ok", "mv_ready", "rs_own", "rstd_ready"))
        max_own, nmax_ready, exp_done, inv_own, hi_own, p_ready = (
            sem(n) for n in ("max_own", "nmax_ready", "exp_done", "inv_own", "hi_own", "p_ready"))
        s_ready, pt_ready, pT_ready, a_ready, y_ready, y_right_ok, y_left_ok = (
            sem(n) for n in ("s_ready", "pt_ready", "pT_ready", "a_ready", "y_ready", "y_right_ok", "y_left_ok"))
        x1_ready, nmean_ready, var1_ready, x1b_ready, rs1_own, rstd1_ready, out_ready = (
            sem(n) for n in ("x1_ready", "nmean_ready", "var1_ready", "x1b_ready", "rs1_own", "rstd1_ready", "out_ready"))

        def all_tiles(eng, step, prep_rows, prep_cols, prep_product):
            prep_rows(0)
            prep_cols(0)
            prep_product(0)
            for k in (-2, -1):
                step(k, k)
            for k in range(HB):
                step(k, k)
            with eng.Fori(0, B - 1) as n:
                for k in range(HB, 2 * HB):
                    step(n * TB + k, k)
                    if k == HB:
                        prep_rows(n + 1)
                    if k == PREP:
                        prep_cols(n + 1)
                prep_product(n + 1)
                for k in range(2 * HB, 3 * HB):
                    step(n * TB + k, k)
            for k in range(HB, 2 * HB + 1):
                step((B - 1) * TB + k, k)

        def real(t):
            return not isinstance(t, int) or 0 <= t < T

        def first(t, n):
            return isinstance(t, int) and t < n

        def x_landed(eng, t, k):
            eng.wait_ge(ld_x[k % XRING // UNIT], 16 * (unit_turn(t, k, XRING) + 1))

        def next_batch(t, k):
            return (t - k + 2 * HB) // TB

        def unit_turn(t, k, ring):
            return t // ring if isinstance(t, int) else (t - k % ring) // ring

        block = stack.enter_context(nc.Block())

        @block.sync
        def _(sp):
            def ready(v):
                return v if isinstance(v, int) else sp.snap(v)

            def load_x(u, slot):
                sp.dma_start(x_sb[:, UNIT * slot:UNIT * slot + UNIT, :],
                             x_units[bass.ds(u, 1)].rearrange("o p n d -> p (o n) d")).then_inc(ld_x[slot], 16)

            def load_ctx(n):
                sp.dma_start(c_rows[:, :], ctx_in[bass.ds(n, 1)].rearrange("o v d -> (o v) d")).then_inc(ld_ctx, 16)

            def stack_rows(n):
                if isinstance(n, int):
                    sp.wait_ge(zeroed, 1)
                else:
                    sp.wait_ge(y_ready, TB * n)
                sp.wait_ge(v_hi_ok, 2 * n + 2)
                sp.wait_ge(v_lo_ok, 2 * n + 2)
                hi, lo, to = v_hi[:, :].bitcast(F32), v_lo[:, :].bitcast(F32), stacks[:, :, :].bitcast(F32)
                sp.dma_start(to[0:V, 0, :], lo[:, :]).then_inc(stacked, 16)
                sp.dma_start(to[V:K2, 0, :], hi[0:CUT, :]).then_inc(stacked, 16)
                sp.dma_start(to[0:V - CUT, 1, :], hi[CUT:V, :]).then_inc(stacked, 16)
                sp.dma_start(to[V - CUT:K2 - 1, 1, :], hi[:, :]).then_inc(stacked, 16)

            def unit(u, k, load):
                o, i = k % (ORING // UNIT), k % (XRING // UNIT)
                u = ready(u)
                u_load = ready(u + XRING // UNIT) if load else None
                sp.wait_ge(out_ready, UNIT * u + UNIT)
                sp.dma_start(out_units[bass.ds(u, 1)].rearrange("o p n d -> p (o n) d"),
                             o_sb[:, UNIT * o:UNIT * o + UNIT, :]).then_inc(st_o[o], 16)
                if load:
                    load_x(u_load, i)

            for w in range(2):
                sp.dma_start(w_rows[:, 2 * w:2 * w + 2, :],
                             W.rearrange("(c p) d -> p c d", p=P)[:, 2 * w:2 * w + 2, :]).then_inc(ld_w, 16)
            for u in range(XRING // UNIT):
                load_x(u, u)
            stack_rows(0)
            NU = TB // UNIT
            with sp.Fori(0, B - 1) as n:
                for k in range(NU):
                    if k == 1:
                        n_load = ready(n + 1)
                        sp.wait_ge(v_lo_ok, 2 * n + 2)
                        load_ctx(n_load)
                    if k == NU - 1:
                        stack_rows(n + 1)
                    unit(n * NU + k, k, True)
            for k in range(NU):
                unit((B - 1) * NU + k, k, k < NU - XRING // UNIT)
            for s in st_o:
                sp.wait_ge(s, 16 * (T // ORING))

        @block.gpsimd
        def _(pool):
            pool.memset(ident[:, :], 0.0).then_inc(ident_ok, 1)
            pool.memset(half_neg[:, :], -0.5).then_inc(ident_ok, 1)
            pool.memset(eps[:, :], EPS).then_inc(ident_ok, 1)
            pool.wait_ge(ident_ok, 3)
            pool.affine_select(out=ident[:, :], in_=ident[:, :], compare_op=ALU.not_equal, fill=1.0,
                               base=0, pattern=[[-1, P]], channel_multiplier=1).then_inc(ident_ok, 1)
            pool.memset(stacks[:, :, :].bitcast(F32), 0.0).then_inc(zeroed, 1)
            pool.memset(wc[:, :, :, D + V:D + VP].bitcast(F32), 0.0).then_inc(zeroed, 1)

            def step(t, k):
                if real(t - 1):
                    j, q = (k - 1) % 2, (k - 1) % 4
                    if first(t - 1, 1):
                        pool.wait_ge(biasg_ok, 1)
                    pool.wait_ge(x1_ready, t)
                    if not first(t, 3):
                        pool.wait_ge(out_ready, t - 2)
                    pool.tensor_tensor(x1_bias[:, j, :], x1[:, j, :], bias_g[:, :], ALU.add).then_inc(x1b_ready, 1)
                    pool.wait_ge(var1_ready, t)
                    pool.tensor_tensor(var1_eps[:, q:q + 1], x1_var[:, q:q + 1], eps[:, :], ALU.add)\
                        .then_inc(rs1_own, 1)
                    pool.wait_ge(rs1_own, t)
                    pool.tensor_tensor(rstd1[:, q:q + 1], var1_eps[:, q:q + 1], half_neg[:, :], ALU.pow)\
                        .then_inc(rstd1_ready, 1)
                if real(t + 2):
                    q = (k + 2) % 4
                    pool.wait_ge(mv_ready, t + 3)
                    pool.tensor_tensor(var_eps[:, q:q + 1], mv[:, q, 1:2], eps[:, :], ALU.add).then_inc(rs_own, 1)
                    pool.wait_ge(rs_own, t + 3)
                    pool.tensor_tensor(rstd[:, q:q + 1], var_eps[:, q:q + 1], half_neg[:, :], ALU.pow)\
                        .then_inc(rstd_ready, 1)

            def prep(n):
                pass

            all_tiles(pool, step, prep, prep, prep)

        @block.scalar
        def _(act):
            act.dma_start(ldt_sb[:, :], ld_t).then_inc(ld_low, 16)
            act.dma_start(lut_sb[:, :], lu_t).then_inc(ld_low, 16)
            act.dma_start(down_sb[:, :], down).then_inc(ld_low, 16)
            act.dma_start(upt_sb[:, :], up_t).then_inc(ld_low, 16)
            act.dma_start(gates[:, 0:1], g_xattn.partition_broadcast(P)).then_inc(ld_gate, 16)
            act.dma_start(gates[:, 1:2], g_ffn.partition_broadcast(P)).then_inc(ld_gate, 16)
            act.dma_start(c_rows[:, :], ctx_in[0]).then_inc(ld_ctx, 16)
            act.dma_start(bias[:, :], b.partition_broadcast(P)).then_inc(ld_bias, 16)
            act.wait_ge(ld_gate, 32)
            act.activation(tg[:, :], gates[:, :], ACT.Tanh).then_inc(tg_ok, 1)
            act.wait_ge(low_mm, 1)
            act.activation(l1_sb[:, :], a_ps[0:R_, :], ACT.Copy).then_inc(low_sb, 1)
            act.wait_ge(low_mm, 2)
            act.activation(l2_sb[:, :], a_ps[0:U, :], ACT.Copy).then_inc(low_sb, 1)
            act.wait_ge(ld_bias, 16)
            act.wait_ge(tg_ok, 1)
            act.activation(bias_g[:, :], bias[:, :], ACT.Copy, scale=tg[:, 1:2]).then_inc(biasg_ok, 1)

            def prep_rows(n):
                act.wait_ge(ld_ctx, 16 * n + 16)
                if not isinstance(n, int):
                    act.wait_ge(stacked, 64 * n)
                act.activation(v_hi[:, 0:D], c_rows[:, :], ACT.Copy, scale=tg[0:V, 0:1]).then_inc(v_hi_ok, 1)

            def prep_cols(n):
                act.wait_ge(c_tr, n + 1)
                act.activation(ct[:, 0, :, :], ct_ps, ACT.Copy).then_inc(ct_hi_ok, 1)
                if isinstance(n, int):
                    for c in range(KC):
                        act.wait_ge(w_tr, c + 1)
                        act.activation(wc[:, c, 0, 0:D], w_bank(c), ACT.Copy).then_inc(w_hi_ok, 1)

            def prep_product(n):
                if isinstance(n, int):
                    act.wait_ge(zeroed, 2)
                else:
                    act.wait_ge(s_ready, TB * n)
                act.wait_ge(ct_lo_ok, n + 1)
                for part in range(2):
                    act.activation(wc[:, :, part, D:D + V], ct[:, part, :, :].bitcast(F32), ACT.Copy).then_inc(c_cols, 1)
                if isinstance(n, int):
                    product_rows(n)

            def product_rows(n):
                act.wait_ge(cw_mm, n + 1)
                act.activation(v_hi[:, D:2 * D], c_ps[0:V, :], ACT.Copy, scale=tg[0:V, 0:1]).then_inc(v_hi_ok, 1)

            def step(t, k):
                if real(t - 1):
                    act.wait_ge(pt_ready, t)
                    if not first(t, 2):
                        act.wait_ge(y_ready, t - 1)
                    act.activation(pT[:, :, :], p_transposed((k - 1) % 2), ACT.Copy).then_inc(pT_ready, 1)
                if real(t + 1):
                    j = (k + 1) % 2
                    act.wait_ge(xt_ready, t + 2)
                    if not first(t, 1):
                        act.wait_ge(x_done, t)
                    act.activation(xT[:, j, 0, :, :], xt_ps[:, j, :, :], ACT.Copy).then_inc(xh_ready, 1)
                if real(t):
                    j = k % 2
                    act.wait_ge(nmax_ready, t + 1)
                    act.activation(expd[:, j, :], scores(j), ACT.Exp, bias=neg_max[:, j:j + 1],
                                   scale=rstd[:, k % 4:k % 4 + 1], accum_out=e_sum[:, j:j + 1]).then_inc(exp_done, 1)
                if real(t - 1):
                    j, q = (k - 1) % 2, (k - 1) % 4
                    act.wait_ge(y_ready, t)
                    if not first(t, 3):
                        act.wait_ge(out_ready, t - 2)
                    act.activation(y_sb[:, j, H:D], y_ps[:, j, 1, 0:H], ACT.Copy).then_inc(y_right_ok, 1)
                    act.activation(y_sb[:, j, 0:H], y_ps[:, j, 0, 0:H], ACT.Copy).then_inc(y_left_ok, 1)
                    act.wait_ge(nmean_ready, t)
                    if not first(t, 2):
                        act.wait_ge(var1_ready, t - 1)
                    act.activation(squares[:, :], x1[:, j, :], ACT.Square, bias=x1_nmean[:, j:j + 1], scale=D ** -0.5,
                                   accum_out=x1_var[:, q:q + 1]).then_inc(var1_ready, 1)
                if k == 2 * HB and not isinstance(t, int):
                    product_rows(next_batch(t, k))

            all_tiles(act, step, prep_rows, prep_cols, prep_product)

        @block.tensor
        def _(pe):
            pe.wait_ge(ld_low, 64)
            pe.matmul(a_ps[0:R_, :], ldt_sb[:, :], down_sb[:, :], start=True, stop=True).then_inc(low_mm, 1)
            pe.wait_ge(low_sb, 1)
            pe.matmul(a_ps[0:U, :], lut_sb[:, :], l1_sb[:, :], start=True, stop=True).then_inc(low_mm, 1)
            pe.wait_ge(low_sb, 2)
            for c in range(KC):
                pe.matmul(w_bank(c), upt_sb[:, c * P:(c + 1) * P], l2_sb[:, :],
                          start=True, stop=True).then_inc(low_mm, 1)

            def prep_rows(n):
                pass

            def prep_cols(n):
                pe.wait_ge(c_centred, n + 1)
                if isinstance(n, int):
                    pe.wait_ge(ident_ok, 4)
                else:
                    pe.wait_ge(v_lo_ok, 2 * n)
                for c in range(KC):
                    mm = pe.transpose(ct_ps[:, c, :], c_cent[:, c * P:(c + 1) * P], ident[0:V, 0:V])
                mm.then_inc(c_tr, 1)
                if isinstance(n, int):
                    pe.wait_ge(w_centred, KC)
                    for c in range(KC):
                        for o in range(KC):
                            mm = pe.transpose(w_bank(c)[:, o * P:(o + 1) * P], w_cent[:, o, c * P:(c + 1) * P], ident[:, :])
                        mm.then_inc(w_tr, 1)

            def prep_product(n):
                pe.wait_ge(ct_hi_ok, n + 1)
                pe.wait_ge(ct_lo_ok, n + 1)
                if isinstance(n, int):
                    pe.wait_ge(w_lo_ok, KC)
                m = 0
                for c in range(KC):
                    for lhs, rhs in ((0, 0), (0, 1), (1, 0)):
                        mm = pe.matmul(c_ps[0:V, :], ct[:, lhs, c, :], wc[:, c, rhs, 0:D],
                                       start=(m == 0), stop=(m == 3 * KC - 1))
                        m += 1
                mm.then_inc(cw_mm, 1)

            def x_transposes(t, k):
                x_landed(pe, t, k)
                if not first(t, 2):
                    pe.wait_ge(xl_ready, t - 1)
                for c in range(KC):
                    mm = pe.transpose(xt_ps[:, k % 2, c, :], x_sb[:, k % XRING, c * P:(c + 1) * P], ident[:, :])
                mm.then_inc(xt_ready, 1)

            def x_product(t, k, h, chunks):
                n = H if h == 0 else H + VP
                for c in chunks:
                    for part, w in ((0, 0), (0, 1), (1, 0)):
                        mm = pe.matmul(y_ps[:, k % 2, h, 0:n], xT[:, k % 2, part, c, :], wc[:, c, w, h * H:h * H + n],
                                       start=(c == 0 and part == 0 and w == 0),
                                       stop=(c == KC - 1 and part == 1), skip_group_check=True)
                if c == KC - 1:
                    mm.then_inc(s_ready if h == 1 else x_done, 1)

            def p_transposes(t, k):
                pe.wait_ge(p_ready, t + 1)
                for s in range(2):
                    mm = pe.matmul(p_transposed(k % 2)[:, s, :], p_ext[:, s * K2:(s + 1) * K2], ident[:, :],
                                   is_transpose=True, start=False, stop=True, skip_group_check=True)
                mm.then_inc(pt_ready, 1)

            def p_product(t, k):
                pe.wait_ge(pT_ready, t + 1)
                if k % TB == 0:
                    pe.wait_ge(stacked, 64 * (t // TB + 1) if isinstance(t, int) else 4 * (t + TB))
                if not first(t, 1):
                    pe.wait_ge(x1_ready, t)
                for s in range(2):
                    mm = pe.matmul(a_ps[:, :], pT[:, s, :], stacks[:, s, 0:D], start=(s == 0), stop=(s == 1))
                mm.then_inc(a_ready, 1)
                for h in (1, 0):
                    for s in range(2):
                        mm = pe.matmul(y_ps[:, k % 2, h, 0:H], pT[:, s, :], stacks[:, s, D + h * H:D + (h + 1) * H],
                                       start=False, stop=(s == 1), skip_group_check=True)
                mm.then_inc(y_ready, 1)

            def step(t, k):
                if real(t):
                    pe.wait_ge(xl_ready, t + 1)
                    if not first(t, 2):
                        pe.wait_ge(y_right_ok, t - 1)
                    if k % TB == 0:
                        pe.wait_ge(c_cols, 2 * (t // TB) + 2 if isinstance(t, int) else (t + TB) // (TB // 2))
                    x_product(t, k, 1, range(KC - 1))
                if real(t - 1):
                    p_transposes(t - 1, k - 1)
                if real(t + 1):
                    x_transposes(t + 1, k + 1)
                if real(t):
                    x_product(t, k, 1, range(KC - 1, KC))
                if real(t - 1):
                    p_product(t - 1, k - 1)
                if real(t):
                    if not first(t, 2):
                        pe.wait_ge(y_left_ok, t - 1)
                    x_product(t, k, 0, range(KC))

            all_tiles(pe, step, prep_rows, prep_cols, prep_product)

        @block.vector
        def _(dve):
            dve.memset(p_ext[:, :], 0.0).then_inc(hi_own, 1)

            def prep_rows(n):
                dve.wait_ge(ld_ctx, 16 * n + 16)
                dve.bn_stats(c_bn[:, :], c_rows[:, :]).then_inc(c_own, 1)
                if isinstance(n, int):
                    dve.wait_ge(tg_ok, 1)
                dve.wait_ge(c_own, 2 * n + 1)
                dve.wait_ge(v_hi_ok, 2 * n + 1)
                dve.scalar_tensor_tensor(out=v_lo[:, 0:D], in0=c_rows[:, :], scalar=tg[0:V, 0:1],
                                         in1=v_hi[:, 0:D].bitcast(F32), op0=ALU.mult, op1=ALU.subtract)\
                    .then_inc(v_lo_ok, 1)
                dve.bn_aggr(c_mv[:, :], c_bn[:, :]).then_inc(c_own, 1)
                dve.wait_ge(c_own, 2 * n + 2)
                dve.tensor_scalar(c_cent[:, :], c_rows[:, :], c_mv[:, 0:1], None, ALU.subtract).then_inc(c_centred, 1)

            def prep_cols(n):
                if isinstance(n, int):
                    centre_w()
                dve.wait_ge(ct_hi_ok, n + 1)
                dve.tensor_tensor(ct[:, 1, :, :], ct_ps, ct[:, 0, :, :].bitcast(F32), ALU.subtract)\
                    .then_inc(ct_lo_ok, 1)
                if isinstance(n, int):
                    for c in range(KC):
                        dve.wait_ge(w_hi_ok, c + 1)
                        dve.tensor_tensor(wc[:, c, 1, 0:D], w_bank(c), wc[:, c, 0, 0:D].bitcast(F32),
                                          ALU.subtract).then_inc(w_lo_ok, 1)

            def centre_w():
                dve.wait_ge(ld_w, 32)
                for c in range(KC):
                    dve.wait_ge(low_mm, 3 + c)
                    dve.tensor_tensor(w_sum[:, c, :], w_bank(c), w_rows[:, c, :], ALU.add).then_inc(w_own, 1)
                for c in range(KC):
                    dve.wait_ge(w_own, c + 1)
                    dve.bn_stats(w_bn[:, c, :], w_sum[:, c, :]).then_inc(w_own, 1)
                for c in range(KC):
                    dve.wait_ge(w_own, KC + c + 1)
                    dve.bn_aggr(w_mv[:, c, :], w_bn[:, c, :]).then_inc(w_own, 1)
                for c in range(KC):
                    dve.wait_ge(w_own, 2 * KC + c + 1)
                    dve.tensor_scalar(w_cent[:, c, :], w_sum[:, c, :], w_mv[:, c, 0:1], tg[:, 1:2],
                                      ALU.subtract, ALU.mult).then_inc(w_centred, 1)

            def prep_product(n):
                if isinstance(n, int):
                    product_rows(n)

            def product_rows(n):
                dve.wait_ge(v_hi_ok, 2 * n + 2)
                dve.scalar_tensor_tensor(out=v_lo[:, D:2 * D], in0=c_ps[0:V, :], scalar=tg[0:V, 0:1],
                                         in1=v_hi[:, D:2 * D].bitcast(F32), op0=ALU.mult, op1=ALU.subtract)\
                    .then_inc(v_lo_ok, 1)

            p_pair = p_ext[:, :].rearrange("p (a v) -> p a v", a=2)[:, :, 0:V].bitcast(F32R)

            def step(t, k):
                j, i = k % 2, (k - 1) % 2
                if real(t + 1):
                    dve.wait_ge(xh_ready, t + 2)
                    dve.tensor_tensor(xT[:, i, 1, :, :], xt_ps[:, i, :, :], xT[:, i, 0, :, :].bitcast(F32),
                                      ALU.subtract).then_inc(xl_ready, 1)
                if real(t):
                    dve.wait_ge(s_ready, t + 1)
                    dve.reduce_max(s_max[:, j:j + 1], scores(j), AX.X).then_inc(max_own, 1)
                    dve.wait_ge(max_own, t + 1)
                    dve.wait_ge(rstd_ready, t + 1)
                    dve.tensor_scalar(neg_max[:, j:j + 1], s_max[:, j:j + 1], rstd[:, k % 4:k % 4 + 1], -1.0,
                                      ALU.mult, ALU.mult).then_inc(nmax_ready, 1)
                if real(t - 1):
                    dve.wait_ge(a_ready, t)
                    if not first(t, 3):
                        dve.wait_ge(var1_ready, t - 2)
                        dve.wait_ge(x1b_ready, t - 2)
                    dve.scalar_tensor_tensor(out=x1[:, i, :], in0=a_ps[:, :], scalar=1.0,
                                             in1=x_sb[:, (k - 1) % XRING, :], op0=ALU.mult, op1=ALU.add,
                                             accum_out=x1_sum[:, i:i + 1]).then_inc(x1_ready, 1)
                    dve.wait_ge(x1_ready, t)
                    dve.tensor_scalar(x1_nmean[:, i:i + 1], x1_sum[:, i:i + 1], -D ** -1.5, None, ALU.mult)\
                        .then_inc(nmean_ready, 1)
                if real(t):
                    dve.wait_ge(exp_done, t + 1)
                    dve.reciprocal(e_inv[:, j:j + 1], e_sum[:, j:j + 1]).then_inc(inv_own, 1)
                    dve.wait_ge(inv_own, t + 1)
                    if first(t, 1):
                        dve.wait_ge(hi_own, 1)
                    else:
                        dve.wait_ge(pt_ready, t)
                    dve.tensor_scalar(p_pair, expd[:, j:j + 1, :].to_broadcast([P, 2, V]), e_inv[:, j:j + 1], None,
                                      ALU.mult).then_inc(hi_own, 1)
                    dve.wait_ge(hi_own, t + 2)
                    dve.scalar_tensor_tensor(out=p_ext[:, V:2 * V].bitcast(F32R), in0=expd[:, j, :],
                                             scalar=e_inv[:, j:j + 1], in1=p_ext[:, 0:V],
                                             op0=ALU.mult, op1=ALU.subtract).then_inc(p_ready, 1)
                if real(t + 2):
                    x_landed(dve, t + 2, k + 2)
                    dve.bn_stats(bn[:, j, :], x_sb[:, (k + 2) % XRING, :]).then_inc(bn_ok, 1)
                if real(t - 1):
                    q = (k - 1) % 4
                    dve.wait_ge(y_left_ok, t)
                    dve.wait_ge(rstd1_ready, t)
                    dve.wait_ge(x1b_ready, t)
                    if not first(t - 1, ORING):
                        dve.wait_ge(st_o[q // UNIT], 16 * unit_turn(t - 1, k - 1, ORING))
                    if real(t + 2):
                        dve.wait_ge(bn_ok, t + 3)
                    dve.scalar_tensor_tensor(out=o_sb[:, q, :], in0=y_sb[:, i, :], scalar=rstd1[:, q:q + 1],
                                             in1=x1_bias[:, i, :], op0=ALU.mult, op1=ALU.add).then_inc(out_ready, 1)
                elif real(t + 2):
                    dve.wait_ge(bn_ok, t + 3)
                if real(t + 2):
                    dve.bn_aggr(mv[:, (k + 2) % 4, :], bn[:, j, :]).then_inc(mv_ready, 1)
                if k == 2 * HB and not isinstance(t, int):
                    product_rows(next_batch(t, k))

            all_tiles(dve, step, prep_rows, prep_cols, prep_product)


def kernel(x, ctx_1024, g_xattn, g_ffn, L0_ffn_W, L0_ffn_b, L0_ffn_lora_down, L0_ffn_lora_up,
           L0_ffn_down_aux, L0_ffn_up_aux):
    import numpy as np
    import concourse.bacc as bacc
    from concourse.bass_utils import run_bass_kernel_spmd

    nc = bacc.Bacc("TRN2", target_bir_lowering=False, num_devices=1)
    ins = {
        "x": x, "ctx": ctx_1024, "g_xattn": g_xattn, "g_ffn": g_ffn, "w": L0_ffn_W, "b": L0_ffn_b,
        "lora_down_t": np.transpose(L0_ffn_lora_down), "lora_up_t": np.transpose(L0_ffn_lora_up),
        "down_aux": L0_ffn_down_aux, "up_aux_t": np.transpose(L0_ffn_up_aux),
    }
    arrays, args = {}, []
    for name, a in ins.items():
        arrays[f"in_{name}"] = np.ascontiguousarray(a)
        args.append(nc.dram_tensor(f"in_{name}", arrays[f"in_{name}"].shape, mybir.dt.from_np(arrays[f"in_{name}"].dtype),
                                   kind="ExternalInput").ap())
    out = nc.dram_tensor("out", x.shape, F32, kind="ExternalOutput").ap()
    build_kernel(nc, *args, out)
    r = run_bass_kernel_spmd(nc, [arrays], core_ids=[0])
    return r.results[0]["out"]
```

```python
from contextlib import ExitStack

import concourse.bass as bass
from concourse import mybir

F32 = mybir.dt.float32
F32R = mybir.dt.float32r
ALU = mybir.AluOpType
ACT = mybir.ActivationFunctionType
AX = mybir.AxisListType

P = 128
EPS = 1e-5
XRING = 8
UNIT = 2
ORING = 4


def build_kernel(nc, x, ctx_in, W, b_gates, low_in, low_out, out):
    B, S, D = x.shape
    V = ctx_in.shape[1]
    RANK = low_in.shape[1] - D
    U = low_out.shape[0]
    KC = D // P
    TB = S // P
    T = B * TB
    HB = XRING
    STATS, ROWS, CENTRE, TURN, PRODUCT, TAKE, SWITCH = HB, HB + 1, HB + 2, HB + 3, HB + 4, HB + 5, 2 * HB - 1
    H = D // 2
    VP = V + 1
    CUT = V - 32
    K2 = V + CUT
    assert TB == 2 * HB and 2 * K2 >= 3 * V and K2 <= P and D == 512

    x_units = x.rearrange("b (u p n) d -> (b u) p n d", p=P, n=UNIT)
    out_units = out.rearrange("b (u p n) d -> (b u) p n d", p=P, n=UNIT)

    with ExitStack() as stack:
        def sb(name, shape, dt=F32):
            return stack.enter_context(nc.sbuf_tensor(name, shape, dt))

        def ps(name, shape, dt=F32):
            return stack.enter_context(nc.psum_tensor(name, shape, dt))

        def sem(name):
            return stack.enter_context(nc.semaphore(name))

        ident = sb("ident", [P, P])
        b_row = sb("b_row", [P, D + 2])
        tg = sb("tg", [P, 2])
        half_neg = sb("half_neg", [P, 1])
        eps = sb("eps", [P, 1])
        bias_g = sb("bias_g", [P, D])
        low_in_sb = sb("low_in_sb", [low_in.shape[0], RANK + D])
        low_out_sb = sb("low_out_sb", [U, RANK + D])
        up_t_sb = sb("up_t_sb", [RANK, D])
        dn_sb = sb("dn_sb", [RANK, D])
        dn_bn = sb("dn_bn", [RANK, 6])
        dn_mv = sb("dn_mv", [RANK, 2])
        w_rows = sb("w_rows", [P, KC, D])
        w_cent = sb("w_cent", [P, KC, D])
        w_bn = sb("w_bn", [P, KC, 6])
        w_mv = sb("w_mv", [P, KC, 2])
        wc = sb("wc", [P, KC, 2, D + VP], F32R)
        c_rows = sb("c_rows", [V, D])
        c_bn = sb("c_bn", [V, 6])
        c_mv = sb("c_mv", [V, 2])
        c_cent = sb("c_cent", [V, D])
        ct = sb("ct", [P, 2, KC, V], F32R)
        v_hi = sb("v_hi", [V, 2 * D], F32R)
        v_lo = sb("v_lo", [V, 2 * D], F32R)
        stacks = sb("stacks", [K2, 2, 2, 2 * D], F32R)
        x_sb = sb("x_sb", [P, XRING, D])
        xT = sb("xT", [P, 2, 2, KC, P], F32R)
        bn = sb("bn", [P, 2, 6])
        mv = sb("mv", [P, 4, 2])
        var_eps = sb("var_eps", [P, 4])
        rstd = sb("rstd", [P, 4])
        s_max = sb("s_max", [P, 2])
        neg_max = sb("neg_max", [P, 2])
        expd = sb("expd", [P, 2, V])
        e_sum = sb("e_sum", [P, 2])
        e_inv = sb("e_inv", [P, 2])
        p_ext = sb("p_ext", [P, 4 * V])
        pT = sb("pT", [K2, 2, P], F32R)
        x1 = sb("x1", [P, 2, D])
        x1_sum = sb("x1_sum", [P, 2])
        x1_nmean = sb("x1_nmean", [P, 2])
        squares = sb("squares", [P, D])
        x1_var = sb("x1_var", [P, 4])
        var1_eps = sb("var1_eps", [P, 4])
        rstd1 = sb("rstd1", [P, 4])
        y_sb = sb("y_sb", [P, 4, D])
        x1_bias = sb("x1_bias", [P, 4, D])
        o_sb = sb("o_sb", [P, ORING, D])

        y_ps = ps("y_ps", [P, 2, 2, D])
        a_ps = ps("a_ps", [P, D])
        xt_ps = ps("xt_ps", [P, 2, KC, P])
        c_ps = ps("c_ps", [P, D])
        ct_ps = c_ps[:, 0:KC * V].rearrange("p (c v) -> p c v", c=KC)

        def scores(j):
            return y_ps[:, j, 1, H:H + V]

        def p_transposed(j):
            return y_ps[0:K2, j, 0, H:D].rearrange("p (s r) -> p s r", s=2)

        def w_bank(c):
            return y_ps[:, c // 2, c % 2, :]

        ld_x = [sem(f"ld_x{i}") for i in range(XRING // UNIT)]
        st_o = [sem(f"st_o{i}") for i in range(ORING // UNIT)]
        ld_w = [sem(f"ld_w{i}") for i in range(2)]
        ld_b, ld_low, ld_ctx = (sem(n) for n in ("ld_b", "ld_low", "ld_ctx"))
        zeroed, ident_ok, tg_ok, biasg_ok = (sem(n) for n in ("zeroed", "ident_ok", "tg_ok", "biasg_ok"))
        low_mm, dn_own, dn_ok, up_ok = (sem(n) for n in ("low_mm", "dn_own", "dn_ok", "up_ok"))
        w_own, w_centred, w_tr, w_hi_ok, w_lo_ok = (sem(n) for n in ("w_own", "w_centred", "w_tr", "w_hi_ok", "w_lo_ok"))
        c_own, c_centred, c_tr, ct_hi_ok, ct_lo_ok = (sem(n) for n in ("c_own", "c_centred", "c_tr", "ct_hi_ok", "ct_lo_ok"))
        c_cols, cw_mm, v_hi_ok, v_lo_ok = (sem(n) for n in ("c_cols", "cw_mm", "v_hi_ok", "v_lo_ok"))
        stacked = [sem(f"stacked{i}") for i in range(2)]
        xt_ready, xh_ready, xl_ready, x_done = (sem(n) for n in ("xt_ready", "xh_ready", "xl_ready", "x_done"))
        bn_ok, mv_ready, rs_own, rstd_ready = (sem(n) for n in ("bn_ok", "mv_ready", "rs_own", "rstd_ready"))
        max_own, nmax_ready, exp_done, inv_own, hi_own, p_ready = (
            sem(n) for n in ("max_own", "nmax_ready", "exp_done", "inv_own", "hi_own", "p_ready"))
        s_ready, pt_ready, pT_ready, a_ready, y_ready, y_right_ok, y_left_ok = (
            sem(n) for n in ("s_ready", "pt_ready", "pT_ready", "a_ready", "y_ready", "y_right_ok", "y_left_ok"))
        x1_ready, nmean_ready, var1_ready, x1b_ready, rs1_own, rstd1_ready, out_ready = (
            sem(n) for n in ("x1_ready", "nmean_ready", "var1_ready", "x1b_ready", "rs1_own", "rstd1_ready", "out_ready"))

        def all_tiles(eng, step, prep):
            for k in range(-2, HB):
                step(k, k)
            with eng.Fori(0, B - 1) as n:
                for k in range(HB, 2 * HB):
                    step(n * TB + k, k)
                    prep(n + 1, k)
                for k in range(2 * HB, 3 * HB):
                    step(n * TB + k, k)
            for k in range(HB, 2 * HB + 1):
                step((B - 1) * TB + k, k)

        def real(t):
            return not isinstance(t, int) or 0 <= t < T

        def first(t, n):
            return isinstance(t, int) and t < n

        def x_landed(eng, t, k):
            eng.wait_ge(ld_x[k % XRING // UNIT], 16 * (unit_turn(t, k, XRING) + 1))

        def unit_turn(t, k, ring):
            return t // ring if isinstance(t, int) else (t - k % ring) // ring

        block = stack.enter_context(nc.Block())

        @block.sync
        def _(sp):
            def ready(v):
                return v if isinstance(v, int) else sp.snap(v)

            def load_x(u, slot):
                sp.dma_start(x_sb[:, UNIT * slot:UNIT * slot + UNIT, :],
                             x_units[bass.ds(u, 1)].rearrange("o p n d -> p (o n) d")).then_inc(ld_x[slot], 16)

            def load_ctx(n):
                sp.dma_start(c_rows[:, :], ctx_in[bass.ds(n, 1)].rearrange("o v d -> (o v) d")).then_inc(ld_ctx, 16)

            def stack_rows(n, part):
                if isinstance(n, int):
                    sp.wait_ge(zeroed, 1)
                else:
                    sp.wait_ge(y_ready, TB * n - (HB if part == 0 else 0))
                sp.wait_ge(v_hi_ok, 2 * n + 2)
                sp.wait_ge(v_lo_ok, 2 * n + 2)
                hi, lo, to = v_hi[:, :].bitcast(F32), v_lo[:, :].bitcast(F32), stacks[:, part, :, :].bitcast(F32)
                for rows, source in ((to[0:V, 0, :], lo), (to[V:K2, 0, :], hi[0:CUT, :]),
                                     (to[0:V - CUT, 1, :], hi[CUT:V, :]), (to[V - CUT:2 * V - CUT, 1, :], hi)):
                    sp.dma_start(rows, source).then_inc(stacked[part], 16)

            def unit(u, k, load):
                o, i = k % (ORING // UNIT), k % (XRING // UNIT)
                u = ready(u)
                u_load = ready(u + XRING // UNIT) if load else None
                sp.wait_ge(out_ready, UNIT * u + UNIT)
                sp.dma_start(out_units[bass.ds(u, 1)].rearrange("o p n d -> p (o n) d"),
                             o_sb[:, UNIT * o:UNIT * o + UNIT, :]).then_inc(st_o[o], 16)
                if load:
                    load_x(u_load, i)

            sp.dma_start(low_in_sb[:, :], low_in).then_inc(ld_low, 16)
            sp.dma_start(low_out_sb[:, :], low_out).then_inc(ld_low, 16)
            load_x(0, 0)
            for u in range(1, XRING // UNIT):
                load_x(u, u)
            for part in range(2):
                stack_rows(0, part)
            NU = TB // UNIT
            with sp.Fori(0, B - 1) as n:
                for k in range(NU):
                    if k == 1:
                        n_load = ready(n + 1)
                        sp.wait_ge(v_lo_ok, 2 * n + 2)
                        load_ctx(n_load)
                    if k >= NU - 2:
                        stack_rows(n + 1, k - (NU - 2))
                    unit(n * NU + k, k, True)
            for k in range(NU):
                unit((B - 1) * NU + k, k, k < NU - XRING // UNIT)
            for s in st_o:
                sp.wait_ge(s, 16 * (T // ORING))

        @block.gpsimd
        def _(pool):
            pool.memset(ident[:, :], 0.0).then_inc(ident_ok, 1)
            pool.memset(half_neg[:, :], -0.5).then_inc(ident_ok, 1)
            pool.memset(eps[:, :], EPS).then_inc(ident_ok, 1)
            pool.wait_ge(ident_ok, 3)
            pool.affine_select(out=ident[:, :], in_=ident[:, :], compare_op=ALU.not_equal, fill=1.0,
                               base=0, pattern=[[-1, P]], channel_multiplier=1).then_inc(ident_ok, 1)
            pool.memset(stacks[:, :, 1, :].bitcast(F32), 0.0).then_inc(zeroed, 1)
            pool.memset(wc[:, :, :, D + V:D + VP].bitcast(F32), 0.0).then_inc(zeroed, 1)

            def step(t, k):
                if real(t - 1):
                    j, q = (k - 1) % 2, (k - 1) % 4
                    if first(t - 1, 1):
                        pool.wait_ge(biasg_ok, 1)
                    pool.wait_ge(x1_ready, t)
                    if not first(t, 5):
                        pool.wait_ge(out_ready, t - 4)
                    pool.tensor_tensor(x1_bias[:, q, :], x1[:, j, :], bias_g[:, :], ALU.add).then_inc(x1b_ready, 1)
                    pool.wait_ge(var1_ready, t)
                    pool.tensor_tensor(var1_eps[:, q:q + 1], x1_var[:, q:q + 1], eps[:, :], ALU.add)\
                        .then_inc(rs1_own, 1)
                    pool.wait_ge(rs1_own, t)
                    pool.tensor_tensor(rstd1[:, q:q + 1], var1_eps[:, q:q + 1], half_neg[:, :], ALU.pow)\
                        .then_inc(rstd1_ready, 1)
                if real(t + 2):
                    q = (k + 2) % 4
                    pool.wait_ge(mv_ready, t + 3)
                    pool.tensor_tensor(var_eps[:, q:q + 1], mv[:, q, 1:2], eps[:, :], ALU.add).then_inc(rs_own, 1)
                    pool.wait_ge(rs_own, t + 3)
                    pool.tensor_tensor(rstd[:, q:q + 1], var_eps[:, q:q + 1], half_neg[:, :], ALU.pow)\
                        .then_inc(rstd_ready, 1)

            def prep(n, k):
                pass

            all_tiles(pool, step, prep)

        @block.scalar
        def _(act):
            for i in range(2):
                act.dma_start(w_rows[:, 2 * i:2 * i + 2, :],
                              W.rearrange("(c p) d -> p c d", p=P)[:, 2 * i:2 * i + 2, :]).then_inc(ld_w[i], 16)
            act.dma_start(b_row[:, :], b_gates.partition_broadcast(P)).then_inc(ld_b, 16)
            act.dma_start(c_rows[:, :], ctx_in[0]).then_inc(ld_ctx, 16)

            def prep(n, k):
                if k == STATS:
                    act.wait_ge(ld_ctx, 16 * n + 16)
                    if not isinstance(n, int):
                        for s in stacked:
                            act.wait_ge(s, 64 * n)
                    act.activation(v_hi[:, 0:D], c_rows[:, :], ACT.Copy, scale=tg[0:V, 0:1]).then_inc(v_hi_ok, 1)
                if k == TURN:
                    act.wait_ge(c_tr, n + 1)
                    act.activation(ct[:, 0, :, :], ct_ps, ACT.Copy).then_inc(ct_hi_ok, 1)
                if k == TAKE:
                    act.wait_ge(cw_mm, n + 1)
                    act.activation(v_hi[:, D:2 * D], c_ps[0:V, :], ACT.Copy, scale=tg[0:V, 0:1]).then_inc(v_hi_ok, 1)

            def ctx_columns(n):
                if isinstance(n, int):
                    act.wait_ge(zeroed, 2)
                else:
                    act.wait_ge(s_ready, TB * n)
                act.wait_ge(ct_lo_ok, n + 1)
                for part in range(2):
                    act.activation(wc[:, :, part, D:D + V], ct[:, part, :, :].bitcast(F32), ACT.Copy).then_inc(c_cols, 1)

            act.wait_ge(ld_b, 16)
            act.activation(tg[:, :], b_row[:, D:D + 2], ACT.Tanh).then_inc(tg_ok, 1)
            act.wait_ge(low_mm, 2)
            act.activation(up_t_sb[:, :], c_ps[0:RANK, :], ACT.Copy).then_inc(up_ok, 1)
            act.wait_ge(tg_ok, 1)
            prep(0, STATS)
            prep(0, TURN)
            ctx_columns(0)
            act.activation(bias_g[:, :], b_row[:, 0:D], ACT.Copy, scale=tg[:, 1:2]).then_inc(biasg_ok, 1)
            for c in range(KC):
                act.wait_ge(w_tr, c + 1)
                act.activation(wc[:, c, 0, 0:D], w_bank(c), ACT.Copy, scale=tg[:, 1:2]).then_inc(w_hi_ok, 1)

            def step(t, k):
                if real(t - 1):
                    act.wait_ge(pt_ready, t)
                    if not first(t, 2):
                        act.wait_ge(y_ready, t - 1)
                    act.activation(pT[:, :, :], p_transposed((k - 1) % 2), ACT.Copy).then_inc(pT_ready, 1)
                if real(t + 1):
                    j = (k + 1) % 2
                    act.wait_ge(xt_ready, t + 2)
                    if not first(t, 1):
                        act.wait_ge(x_done, t)
                    act.activation(xT[:, j, 0, :, :], xt_ps[:, j, :, :], ACT.Copy).then_inc(xh_ready, 1)
                if real(t):
                    j = k % 2
                    act.wait_ge(nmax_ready, t + 1)
                    act.activation(expd[:, j, :], scores(j), ACT.Exp, bias=neg_max[:, j:j + 1],
                                   scale=rstd[:, k % 4:k % 4 + 1], accum_out=e_sum[:, j:j + 1]).then_inc(exp_done, 1)
                if real(t - 1):
                    j, q = (k - 1) % 2, (k - 1) % 4
                    act.wait_ge(y_ready, t)
                    if not first(t, 5):
                        act.wait_ge(out_ready, t - 4)
                    act.activation(y_sb[:, q, H:D], y_ps[:, j, 1, 0:H], ACT.Copy).then_inc(y_right_ok, 1)
                    act.activation(y_sb[:, q, 0:H], y_ps[:, j, 0, 0:H], ACT.Copy).then_inc(y_left_ok, 1)
                if k == SWITCH and not isinstance(t, int):
                    ctx_columns((t - k) // TB + 1)
                if real(t - 1):
                    j, q = (k - 1) % 2, (k - 1) % 4
                    act.wait_ge(nmean_ready, t)
                    if not first(t, 2):
                        act.wait_ge(var1_ready, t - 1)
                    act.activation(squares[:, :], x1[:, j, :], ACT.Square, bias=x1_nmean[:, j:j + 1], scale=D ** -0.5,
                                   accum_out=x1_var[:, q:q + 1]).then_inc(var1_ready, 1)
                if k == 0 and isinstance(t, int):
                    prep(0, TAKE)

            all_tiles(act, step, prep)

        @block.tensor
        def _(pe):
            pe.wait_ge(ld_low, 32)
            pe.matmul(a_ps[0:RANK, :], low_in_sb[:, 0:RANK], low_in_sb[:, RANK:RANK + D], start=True, stop=True)\
                .then_inc(low_mm, 1)
            pe.matmul(c_ps[0:RANK, :], low_out_sb[:, 0:RANK], low_out_sb[:, RANK:RANK + D], start=True, stop=True)\
                .then_inc(low_mm, 1)

            def prep(n, k):
                if k == TURN:
                    pe.wait_ge(c_centred, n + 1)
                    if isinstance(n, int):
                        pe.wait_ge(up_ok, 1)
                        pe.wait_ge(ident_ok, 4)
                    else:
                        pe.wait_ge(v_lo_ok, 2 * n)
                    for c in range(KC):
                        mm = pe.transpose(ct_ps[:, c, :], c_cent[:, c * P:(c + 1) * P], ident[0:V, 0:V])
                    mm.then_inc(c_tr, 1)
                if k == PRODUCT:
                    pe.wait_ge(ct_hi_ok, n + 1)
                    pe.wait_ge(ct_lo_ok, n + 1)
                    if isinstance(n, int):
                        pe.wait_ge(w_lo_ok, KC)
                    m = 0
                    for c in range(KC):
                        for lhs, rhs in ((0, 0), (0, 1), (1, 0)):
                            mm = pe.matmul(c_ps[0:V, :], ct[:, lhs, c, :], wc[:, c, rhs, 0:D],
                                           start=(m == 0), stop=(m == 3 * KC - 1))
                            m += 1
                    mm.then_inc(cw_mm, 1)

            def x_transposes(t, k):
                x_landed(pe, t, k)
                if not first(t, 2):
                    pe.wait_ge(xl_ready, t - 1)
                for c in range(KC):
                    mm = pe.transpose(xt_ps[:, k % 2, c, :], x_sb[:, k % XRING, c * P:(c + 1) * P], ident[:, :])
                mm.then_inc(xt_ready, 1)

            def x_product(t, k, h, chunks):
                n = H if h == 0 else H + VP
                for c in chunks:
                    for part, w in ((0, 0), (0, 1), (1, 0)):
                        mm = pe.matmul(y_ps[:, k % 2, h, 0:n], xT[:, k % 2, part, c, :], wc[:, c, w, h * H:h * H + n],
                                       start=(c == 0 and part == 0 and w == 0),
                                       stop=(c == KC - 1 and part == 1), skip_group_check=True)
                if c == KC - 1:
                    mm.then_inc(s_ready if h == 1 else x_done, 1)

            def p_transposes(t, k):
                pe.wait_ge(p_ready, t + 1)
                for s in range(2):
                    mm = pe.matmul(p_transposed(k % 2)[:, s, :], p_ext[:, s * K2:(s + 1) * K2], ident[:, :],
                                   is_transpose=True, start=False, stop=True, skip_group_check=True)
                mm.then_inc(pt_ready, 1)

            def p_product(t, k):
                pe.wait_ge(pT_ready, t + 1)
                pair = k % TB // HB
                if k % HB == 0:
                    pe.wait_ge(stacked[pair], 64 * (t // TB + 1) if isinstance(t, int) else 4 * (t - k % TB + TB))
                if not first(t, 1):
                    pe.wait_ge(x1_ready, t)
                for s in range(2):
                    mm = pe.matmul(a_ps[:, :], pT[:, s, :], stacks[:, pair, s, 0:D], start=(s == 0), stop=(s == 1))
                mm.then_inc(a_ready, 1)
                for h in (1, 0):
                    for s in range(2):
                        mm = pe.matmul(y_ps[:, k % 2, h, 0:H], pT[:, s, :], stacks[:, pair, s, D + h * H:D + (h + 1) * H],
                                       start=False, stop=(s == 1), skip_group_check=True)
                mm.then_inc(y_ready, 1)

            def step(t, k):
                if first(t, 1) and real(t):
                    prep(0, PRODUCT)
                if real(t):
                    pe.wait_ge(xl_ready, t + 1)
                    if not first(t, 2):
                        pe.wait_ge(y_right_ok, t - 1)
                    if k % TB == 0:
                        pe.wait_ge(c_cols, 2 * (t // TB) + 2 if isinstance(t, int) else (t + TB) // (TB // 2))
                    x_product(t, k, 1, range(KC - 1))
                if real(t - 1):
                    p_transposes(t - 1, k - 1)
                if real(t + 1):
                    x_transposes(t + 1, k + 1)
                if real(t):
                    x_product(t, k, 1, range(KC - 1, KC))
                if real(t - 1):
                    p_product(t - 1, k - 1)
                if real(t):
                    if not first(t, 2):
                        pe.wait_ge(y_left_ok, t - 1)
                    x_product(t, k, 0, range(KC))

            pe.wait_ge(dn_ok, 1)
            pe.wait_ge(up_ok, 1)
            for c in range(KC):
                pe.matmul(w_bank(c), dn_sb[:, c * P:(c + 1) * P], up_t_sb[:, :], start=True, stop=False,
                          skip_group_check=True)
            prep(0, TURN)
            pe.wait_ge(w_centred, KC)
            for c in range(KC):
                for o in range(KC):
                    mm = pe.matmul(w_bank(c)[:, o * P:(o + 1) * P], w_cent[:, o, c * P:(c + 1) * P], ident[:, :],
                                   is_transpose=True, start=False, stop=True, skip_group_check=True)
                mm.then_inc(w_tr, 1)
            all_tiles(pe, step, prep)

        @block.vector
        def _(dve):
            dve.memset(p_ext[:, :], 0.0).then_inc(hi_own, 1)

            def prep(n, k):
                if k == STATS:
                    dve.wait_ge(ld_ctx, 16 * n + 16)
                    dve.bn_stats(c_bn[:, :], c_rows[:, :]).then_inc(c_own, 1)
                if k == ROWS:
                    dve.wait_ge(c_own, 2 * n + 1)
                    dve.wait_ge(v_hi_ok, 2 * n + 1)
                    dve.scalar_tensor_tensor(out=v_lo[:, 0:D], in0=c_rows[:, :], scalar=tg[0:V, 0:1],
                                             in1=v_hi[:, 0:D].bitcast(F32), op0=ALU.mult, op1=ALU.subtract)\
                        .then_inc(v_lo_ok, 1)
                    dve.bn_aggr(c_mv[:, :], c_bn[:, :]).then_inc(c_own, 1)
                if k == CENTRE:
                    dve.wait_ge(c_own, 2 * n + 2)
                    dve.tensor_scalar(c_cent[:, :], c_rows[:, :], c_mv[:, 0:1], None, ALU.subtract)\
                        .then_inc(c_centred, 1)
                if k == TURN:
                    dve.wait_ge(ct_hi_ok, n + 1)
                    dve.tensor_tensor(ct[:, 1, :, :], ct_ps, ct[:, 0, :, :].bitcast(F32), ALU.subtract)\
                        .then_inc(ct_lo_ok, 1)
                if k == TAKE:
                    dve.wait_ge(v_hi_ok, 2 * n + 2)
                    dve.scalar_tensor_tensor(out=v_lo[:, D:2 * D], in0=c_ps[0:V, :], scalar=tg[0:V, 0:1],
                                             in1=v_hi[:, D:2 * D].bitcast(F32), op0=ALU.mult, op1=ALU.subtract)\
                        .then_inc(v_lo_ok, 1)

            def centre_w(half):
                dve.wait_ge(ld_w[half], 16)
                mine = range(2 * half, 2 * half + 2)
                for c in mine:
                    dve.bn_stats(w_bn[:, c, :], w_rows[:, c, :]).then_inc(w_own, 1)
                for c in mine:
                    dve.wait_ge(w_own, 2 * half + c + 1)
                    dve.bn_aggr(w_mv[:, c, :], w_bn[:, c, :]).then_inc(w_own, 1)
                for c in mine:
                    dve.wait_ge(w_own, 2 * half + 2 + c + 1)
                    dve.tensor_scalar(w_cent[:, c, :], w_rows[:, c, :], w_mv[:, c, 0:1], None, ALU.subtract)\
                        .then_inc(w_centred, 1)

            centre_w(0)
            dve.wait_ge(low_mm, 1)
            dve.bn_stats(dn_bn[:, :], a_ps[0:RANK, :]).then_inc(dn_own, 1)
            dve.wait_ge(dn_own, 1)
            dve.bn_aggr(dn_mv[:, :], dn_bn[:, :]).then_inc(dn_own, 1)
            dve.wait_ge(dn_own, 2)
            dve.tensor_scalar(dn_sb[:, :], a_ps[0:RANK, :], dn_mv[:, 0:1], None, ALU.subtract).then_inc(dn_ok, 1)
            centre_w(1)
            dve.wait_ge(tg_ok, 1)
            for k in (STATS, ROWS, CENTRE, TURN):
                prep(0, k)
            for c in range(KC):
                dve.wait_ge(w_hi_ok, c + 1)
                dve.scalar_tensor_tensor(out=wc[:, c, 1, 0:D], in0=w_bank(c), scalar=tg[:, 1:2],
                                         in1=wc[:, c, 0, 0:D].bitcast(F32), op0=ALU.mult, op1=ALU.subtract)\
                    .then_inc(w_lo_ok, 1)

            p_pair = p_ext[:, :].rearrange("p (a v) -> p a v", a=2)[:, :, 0:V].bitcast(F32R)

            def output(t, k):
                q = k % 4
                dve.wait_ge(y_left_ok, t + 1)
                dve.wait_ge(rstd1_ready, t + 1)
                dve.wait_ge(x1b_ready, t + 1)
                if not first(t, ORING):
                    dve.wait_ge(st_o[q // UNIT], 16 * unit_turn(t, k, ORING))
                dve.scalar_tensor_tensor(out=o_sb[:, q, :], in0=y_sb[:, q, :], scalar=rstd1[:, q:q + 1],
                                         in1=x1_bias[:, q, :], op0=ALU.mult, op1=ALU.add).then_inc(out_ready, 1)

            def step(t, k):
                j, i = k % 2, (k - 1) % 2
                if real(t):
                    dve.wait_ge(s_ready, t + 1)
                    dve.reduce_max(s_max[:, j:j + 1], scores(j), AX.X).then_inc(max_own, 1)
                    dve.wait_ge(max_own, t + 1)
                    dve.wait_ge(rstd_ready, t + 1)
                    dve.tensor_scalar(neg_max[:, j:j + 1], s_max[:, j:j + 1], rstd[:, k % 4:k % 4 + 1], -1.0,
                                      ALU.mult, ALU.mult).then_inc(nmax_ready, 1)
                if real(t + 1):
                    dve.wait_ge(xh_ready, t + 2)
                    dve.tensor_tensor(xT[:, i, 1, :, :], xt_ps[:, i, :, :], xT[:, i, 0, :, :].bitcast(F32),
                                      ALU.subtract).then_inc(xl_ready, 1)
                if real(t):
                    dve.wait_ge(exp_done, t + 1)
                    dve.reciprocal(e_inv[:, j:j + 1], e_sum[:, j:j + 1]).then_inc(inv_own, 1)
                    dve.wait_ge(inv_own, t + 1)
                    if first(t, 1):
                        dve.wait_ge(hi_own, 1)
                    else:
                        dve.wait_ge(pt_ready, t)
                    dve.tensor_scalar(p_pair, expd[:, j:j + 1, :].to_broadcast([P, 2, V]), e_inv[:, j:j + 1], None,
                                      ALU.mult).then_inc(hi_own, 1)
                    dve.wait_ge(hi_own, t + 2)
                    dve.scalar_tensor_tensor(out=p_ext[:, V:2 * V].bitcast(F32R), in0=expd[:, j, :],
                                             scalar=e_inv[:, j:j + 1], in1=p_ext[:, 0:V],
                                             op0=ALU.mult, op1=ALU.subtract).then_inc(p_ready, 1)
                if real(t - 1):
                    dve.wait_ge(a_ready, t)
                    if not first(t, 3):
                        dve.wait_ge(var1_ready, t - 2)
                        dve.wait_ge(x1b_ready, t - 2)
                    dve.scalar_tensor_tensor(out=x1[:, i, :], in0=a_ps[:, :], scalar=1.0,
                                             in1=x_sb[:, (k - 1) % XRING, :], op0=ALU.mult, op1=ALU.add,
                                             accum_out=x1_sum[:, i:i + 1]).then_inc(x1_ready, 1)
                    dve.wait_ge(x1_ready, t)
                    dve.tensor_scalar(x1_nmean[:, i:i + 1], x1_sum[:, i:i + 1], -D ** -1.5, None, ALU.mult)\
                        .then_inc(nmean_ready, 1)
                if real(t + 2):
                    x_landed(dve, t + 2, k + 2)
                    dve.bn_stats(bn[:, j, :], x_sb[:, (k + 2) % XRING, :]).then_inc(bn_ok, 1)
                if real(t + 2):
                    dve.wait_ge(bn_ok, t + 3)
                if real(t - 2):
                    output(t - 2, k - 2)
                if real(t + 2):
                    dve.bn_aggr(mv[:, (k + 2) % 4, :], bn[:, j, :]).then_inc(mv_ready, 1)
                if first(t, 1) and real(t):
                    prep(0, TAKE)

            all_tiles(dve, step, prep)
            output(T - 1, TB - 1)


def kernel(x, ctx_1024, g_xattn, g_ffn, L0_ffn_W, L0_ffn_b, L0_ffn_lora_down, L0_ffn_lora_up,
           L0_ffn_down_aux, L0_ffn_up_aux):
    import numpy as np
    import concourse.bacc as bacc
    from concourse.bass_utils import run_bass_kernel_spmd

    nc = bacc.Bacc("TRN2", target_bir_lowering=False, num_devices=1)
    ins = {
        "x": x, "ctx": ctx_1024, "w": L0_ffn_W,
        "b_gates": np.concatenate([L0_ffn_b, g_xattn, g_ffn]),
        "low_in": np.concatenate([np.transpose(L0_ffn_lora_down), L0_ffn_down_aux], axis=1),
        "low_out": np.concatenate([L0_ffn_lora_up, np.transpose(L0_ffn_up_aux)], axis=1),
    }
    arrays, args = {}, []
    for name, a in ins.items():
        arrays[f"in_{name}"] = np.ascontiguousarray(a)
        args.append(nc.dram_tensor(f"in_{name}", arrays[f"in_{name}"].shape, mybir.dt.from_np(arrays[f"in_{name}"].dtype),
                                   kind="ExternalInput").ap())
    out = nc.dram_tensor("out", x.shape, F32, kind="ExternalOutput").ap()
    build_kernel(nc, *args, out)
    r = run_bass_kernel_spmd(nc, [arrays], core_ids=[0])
    return r.results[0]["out"]
```

```python
from contextlib import ExitStack

import concourse.bass as bass
from concourse import mybir

F32 = mybir.dt.float32
F32R = mybir.dt.float32r
ALU = mybir.AluOpType
ACT = mybir.ActivationFunctionType
AX = mybir.AxisListType

P = 128
EPS = 1e-5
XRING = 8
UNIT = 2
ORING = 4


def build_kernel(nc, x, ctx_in, W, b_gates, low_in, low_out, out):
    B, S, D = x.shape
    V = ctx_in.shape[1]
    LR = low_in.shape[1] - D
    U = low_out.shape[0]
    LQ = 32
    KC = D // P
    TB = S // P
    T = B * TB
    HB = XRING
    STATS, ROWS, CENTRE, TURN, PRODUCT, TAKE, SWITCH = HB, HB + 1, HB + 2, HB + 3, HB + 4, HB + 5, 2 * HB - 1
    H = D // 2
    VP = V + 1
    CUT = V - 32
    K2 = V + CUT
    assert TB == 2 * HB and 2 * K2 >= 3 * V and K2 <= P and D == 512

    x_units = x.rearrange("b (u p n) d -> (b u) p n d", p=P, n=UNIT)
    out_units = out.rearrange("b (u p n) d -> (b u) p n d", p=P, n=UNIT)

    with ExitStack() as stack:
        def sb(name, shape, dt=F32):
            return stack.enter_context(nc.sbuf_tensor(name, shape, dt))

        def ps(name, shape, dt=F32):
            return stack.enter_context(nc.psum_tensor(name, shape, dt))

        def sem(name):
            return stack.enter_context(nc.semaphore(name))

        ident = sb("ident", [P, P])
        b_row = sb("b_row", [P, D + 2])
        tg = sb("tg", [P, 2])
        half_neg = sb("half_neg", [P, 1])
        eps = sb("eps", [P, 1])
        bias_g = sb("bias_g", [P, D])
        low_in_sb = sb("low_in_sb", [low_in.shape[0], LR + D])
        low_out_sb = sb("low_out_sb", [U, LR + D])
        up_st = sb("up_st", [LR, D], F32R)
        dn_st = sb("dn_st", [LR, D], F32R)
        dn_bn = sb("dn_bn", [LR, 6])
        dn_mv = sb("dn_mv", [LR, 2])
        w_rows = sb("w_rows", [P, KC, D])
        w_cent = sb("w_cent", [P, KC, D])
        w_bn = sb("w_bn", [P, 2, 6])
        w_mv = sb("w_mv", [P, 2, 2])
        w_nmean = sb("w_nmean", [P, 2])
        wc = sb("wc", [P, KC, 2, D + VP], F32R)
        c_rows = sb("c_rows", [V, D])
        c_bn = sb("c_bn", [V, 6])
        c_mv = sb("c_mv", [V, 2])
        c_cent = sb("c_cent", [V, D])
        ct = sb("ct", [P, 2, KC, V], F32R)
        v_hi = sb("v_hi", [V, 2 * D], F32R)
        v_lo = sb("v_lo", [V, 2 * D], F32R)
        stacks = sb("stacks", [K2, 2, 2, 2 * D], F32R)
        x_sb = sb("x_sb", [P, XRING, D])
        xT = sb("xT", [P, 2, 2, KC, P], F32R)
        bn = sb("bn", [P, 2, 6])
        mv = sb("mv", [P, 4, 2])
        var_eps = sb("var_eps", [P, 4])
        rstd = sb("rstd", [P, 4])
        s_max = sb("s_max", [P, 2])
        neg_max = sb("neg_max", [P, 2])
        expd = sb("expd", [P, 2, V])
        e_sum = sb("e_sum", [P, 2])
        e_inv = sb("e_inv", [P, 2])
        p_ext = sb("p_ext", [P, 4 * V])
        pT = sb("pT", [K2, 2, P], F32R)
        x1 = sb("x1", [P, 2, D])
        x1_sum = sb("x1_sum", [P, 2])
        x1_nmean = sb("x1_nmean", [P, 2])
        squares = sb("squares", [P, D])
        x1_var = sb("x1_var", [P, 4])
        var1_eps = sb("var1_eps", [P, 4])
        rstd1 = sb("rstd1", [P, 4])
        y_sb = sb("y_sb", [P, 4, D])
        x1_bias = sb("x1_bias", [P, 4, D])
        o_sb = sb("o_sb", [P, ORING, D])

        y_ps = ps("y_ps", [P, 2, 2, D])
        a_ps = ps("a_ps", [P, D])
        xt_ps = ps("xt_ps", [P, 2, KC, P])
        c_ps = ps("c_ps", [P, D])
        ct_ps = c_ps[:, 0:KC * V].rearrange("p (c v) -> p c v", c=KC)

        def scores(j):
            return y_ps[:, j, 1, H:H + V]

        def p_transposed(j):
            return y_ps[0:K2, j, 0, H:D].rearrange("p (s r) -> p s r", s=2)

        def cw_ps(n):
            return a_ps[0:V, :] if isinstance(n, int) else c_ps[0:V, :]

        def w_bank(c):
            return y_ps[:, c // 2, c % 2, :]

        ld_x = [sem(f"ld_x{i}") for i in range(XRING // UNIT)]
        st_o = [sem(f"st_o{i}") for i in range(ORING // UNIT)]
        ld_w = [sem(f"ld_w{i}") for i in range(2)]
        ld_b, ld_gates, ld_in, ld_out, ld_ctx = (sem(n) for n in ("ld_b", "ld_gates", "ld_in", "ld_out", "ld_ctx"))
        zeroed, ident_ok, tg_ok, biasg_ok = (sem(n) for n in ("zeroed", "ident_ok", "tg_ok", "biasg_ok"))
        low_mm, dn_own, dn_ok, up_hi_ok, up_ok = (sem(n) for n in ("low_mm", "dn_own", "dn_ok", "up_hi_ok", "up_ok"))
        w_centred = [sem(f"w_centred{i}") for i in range(2)]
        w_own, w_nmean_ok, w_tr, w_hi_ok, w_lo_ok = (sem(n) for n in ("w_own", "w_nmean_ok", "w_tr", "w_hi_ok", "w_lo_ok"))
        c_own, c_centred, c_tr, ct_hi_ok, ct_lo_ok = (sem(n) for n in ("c_own", "c_centred", "c_tr", "ct_hi_ok", "ct_lo_ok"))
        c_cols, cw_mm, v_hi_ok, v_lo_ok = (sem(n) for n in ("c_cols", "cw_mm", "v_hi_ok", "v_lo_ok"))
        stacked = [sem(f"stacked{i}") for i in range(2)]
        xt_ready, xh_ready, xl_ready, x_done = (sem(n) for n in ("xt_ready", "xh_ready", "xl_ready", "x_done"))
        bn_ok, mv_ready, rs_own, rstd_ready = (sem(n) for n in ("bn_ok", "mv_ready", "rs_own", "rstd_ready"))
        max_own, nmax_ready, exp_done, inv_own, hi_own, p_ready = (
            sem(n) for n in ("max_own", "nmax_ready", "exp_done", "inv_own", "hi_own", "p_ready"))
        s_ready, pt_ready, pT_ready, a_ready, y_ready, y_right_ok, y_left_ok = (
            sem(n) for n in ("s_ready", "pt_ready", "pT_ready", "a_ready", "y_ready", "y_right_ok", "y_left_ok"))
        last_x1b_ready = sem("last_x1b_ready")
        x1_ready, nmean_ready, var1_ready, x1b_ready, rs1_own, rstd1_ready, out_ready = (
            sem(n) for n in ("x1_ready", "nmean_ready", "var1_ready", "x1b_ready", "rs1_own", "rstd1_ready", "out_ready"))

        def all_tiles(eng, step, prep):
            for k in range(0, HB):
                step(k, k)
            with eng.Fori(0, B - 1) as n:
                for k in range(HB, 2 * HB):
                    step(n * TB + k, k)
                    prep(n + 1, k)
                for k in range(2 * HB, 3 * HB):
                    step(n * TB + k, k)
            for k in range(HB, 2 * HB + 1):
                step((B - 1) * TB + k, k)

        def real(t):
            return not isinstance(t, int) or 0 <= t < T

        def tail(t):
            return isinstance(t, int) and t == T - 1

        def first(t, n):
            return isinstance(t, int) and t < n

        def x_landed(eng, t, k):
            eng.wait_ge(ld_x[k % XRING // UNIT], 16 * (unit_turn(t, k, XRING) + 1))

        def unit_turn(t, k, ring):
            return t // ring if isinstance(t, int) else (t - k % ring) // ring

        block = stack.enter_context(nc.Block())

        def load_w(eng, half):
            eng.dma_start(w_rows[:, 2 * half:2 * half + 2, :],
                          W.rearrange("(c p) d -> p c d", p=P)[:, 2 * half:2 * half + 2, :]).then_inc(ld_w[half], 16)

        @block.sync
        def _(sp):
            def ready(v):
                return v if isinstance(v, int) else sp.snap(v)

            def load_x(u, slot):
                sp.dma_start(x_sb[:, UNIT * slot:UNIT * slot + UNIT, :],
                             x_units[bass.ds(u, 1)].rearrange("o p n d -> p (o n) d")).then_inc(ld_x[slot], 16)

            def load_ctx(n):
                sp.dma_start(c_rows[:, :], ctx_in[bass.ds(n, 1)].rearrange("o v d -> (o v) d")).then_inc(ld_ctx, 16)

            def stack_rows(n, part):
                if isinstance(n, int):
                    sp.wait_ge(zeroed, 1)
                else:
                    sp.wait_ge(y_ready, TB * n - (HB if part == 0 else 0))
                sp.wait_ge(v_hi_ok, 2 * n + 2)
                hi, lo, to = v_hi[:, :].bitcast(F32), v_lo[:, :].bitcast(F32), stacks[:, part, :, :].bitcast(F32)
                for rows, source in ((to[V:K2, 0, :], hi[0:CUT, :]), (to[0:V - CUT, 1, :], hi[CUT:V, :]),
                                     (to[V - CUT:2 * V - CUT, 1, :], hi)):
                    sp.dma_start(rows, source).then_inc(stacked[part], 16)
                sp.wait_ge(v_lo_ok, 2 * n + 2)
                sp.dma_start(to[0:V, 0, :], lo).then_inc(stacked[part], 16)

            def unit(u, k, load):
                o, i = k % (ORING // UNIT), k % (XRING // UNIT)
                u = ready(u)
                u_load = ready(u + XRING // UNIT) if load else None
                sp.wait_ge(out_ready, UNIT * u + UNIT)
                sp.dma_start(out_units[bass.ds(u, 1)].rearrange("o p n d -> p (o n) d"),
                             o_sb[:, UNIT * o:UNIT * o + UNIT, :]).then_inc(st_o[o], 16)
                if load:
                    load_x(u_load, i)

            sp.dma_start(low_in_sb[:, :], low_in).then_inc(ld_in, 16)
            sp.dma_start(low_out_sb[:, :], low_out).then_inc(ld_out, 16)
            load_w(sp, 1)
            load_x(0, 0)
            for u in range(1, XRING // UNIT):
                load_x(u, u)
            for part in range(2):
                stack_rows(0, part)
            NU = TB // UNIT
            with sp.Fori(0, B - 1) as n:
                for k in range(NU):
                    if k == 1:
                        n_load = ready(n + 1)
                        sp.wait_ge(v_lo_ok, 2 * n + 2)
                        load_ctx(n_load)
                    if k >= NU - 2:
                        stack_rows(n + 1, k - (NU - 2))
                    unit(n * NU + k, k, True)
            for k in range(NU - 1):
                unit((B - 1) * NU + k, k, k < NU - XRING // UNIT)
            for n in range(UNIT):
                t = T - UNIT + n
                sp.wait_ge(out_ready, t + 1)
                sp.dma_start(out_units[T // UNIT - 1][:, n, :], o_sb[:, t % ORING, :]).then_inc(st_o[-1], 16)
            for i, s in enumerate(st_o):
                sp.wait_ge(s, 16 * (T // ORING) + (16 * (UNIT - 1) if i == len(st_o) - 1 else 0))

        @block.gpsimd
        def _(pool):
            pool.memset(ident[:, :], 0.0).then_inc(ident_ok, 1)
            pool.memset(half_neg[:, :], -0.5).then_inc(ident_ok, 1)
            pool.memset(eps[:, :], EPS).then_inc(ident_ok, 1)
            pool.wait_ge(ident_ok, 3)
            pool.affine_select(out=ident[:, :], in_=ident[:, :], compare_op=ALU.not_equal, fill=1.0,
                               base=0, pattern=[[-1, P]], channel_multiplier=1).then_inc(ident_ok, 1)
            pool.memset(stacks[:, :, 1, :].bitcast(F32), 0.0).then_inc(zeroed, 1)
            pool.memset(wc[:, :, :, D + V:D + VP].bitcast(F32), 0.0).then_inc(zeroed, 1)

            def step(t, k):
                if real(t - 1) and real(t):
                    j, q = (k - 1) % 2, (k - 1) % 4
                    if first(t - 1, 1):
                        pool.wait_ge(biasg_ok, 1)
                    pool.wait_ge(x1_ready, t)
                    if not first(t, 5):
                        pool.wait_ge(out_ready, t - 4)
                    pool.tensor_tensor(x1_bias[:, q, :], x1[:, j, :], bias_g[:, :], ALU.add).then_inc(x1b_ready, 1)
                if real(t - 1):
                    q = (k - 1) % 4
                    pool.wait_ge(var1_ready, t)
                    pool.tensor_tensor(var1_eps[:, q:q + 1], x1_var[:, q:q + 1], eps[:, :], ALU.add)\
                        .then_inc(rs1_own, 1)
                    pool.wait_ge(rs1_own, t)
                    pool.tensor_tensor(rstd1[:, q:q + 1], var1_eps[:, q:q + 1], half_neg[:, :], ALU.pow)\
                        .then_inc(rstd1_ready, 1)
                if real(t + 2):
                    q = (k + 2) % 4
                    pool.wait_ge(mv_ready, t + 3)
                    pool.tensor_tensor(var_eps[:, q:q + 1], mv[:, q, 1:2], eps[:, :], ALU.add).then_inc(rs_own, 1)
                    pool.wait_ge(rs_own, t + 3)
                    pool.tensor_tensor(rstd[:, q:q + 1], var_eps[:, q:q + 1], half_neg[:, :], ALU.pow)\
                        .then_inc(rstd_ready, 1)

            def prep(n, k):
                pass

            for k in (-2, -1):
                step(k, k)
            all_tiles(pool, step, prep)

        @block.scalar
        def _(act):
            load_w(act, 0)
            act.dma_start(c_rows[:, :], ctx_in[0]).then_inc(ld_ctx, 16)
            act.dma_start(b_row[:, D:D + 2], b_gates[D:D + 2].partition_broadcast(P)).then_inc(ld_gates, 16)
            act.dma_start(b_row[:, 0:D], b_gates[0:D].partition_broadcast(P)).then_inc(ld_b, 16)

            def ctx_rows_hi(n):
                act.wait_ge(ld_ctx, 16 * n + 16)
                if isinstance(n, int):
                    act.wait_ge(tg_ok, 1)
                else:
                    for s in stacked:
                        act.wait_ge(s, 64 * n)
                act.activation(v_hi[:, 0:D], c_rows[:, :], ACT.Copy, scale=tg[0:V, 0:1]).then_inc(v_hi_ok, 1)

            def ctx_product_hi(n):
                act.wait_ge(cw_mm, n + 1)
                act.activation(v_hi[:, D:2 * D], cw_ps(n), ACT.Copy, scale=tg[0:V, 0:1]).then_inc(v_hi_ok, 1)

            def prep(n, k):
                if k == TURN:
                    act.wait_ge(c_tr, n + 1)
                    act.activation(ct[:, 0, :, :], ct_ps, ACT.Copy).then_inc(ct_hi_ok, 1)

            def ctx_columns(n):
                if isinstance(n, int):
                    act.wait_ge(zeroed, 2)
                else:
                    act.wait_ge(s_ready, TB * n)
                act.wait_ge(ct_lo_ok, n + 1)
                for part in range(2):
                    act.activation(wc[:, :, part, D:D + V], ct[:, part, :, :].bitcast(F32), ACT.Copy).then_inc(c_cols, 1)

            def evacuate(t, k):
                act.wait_ge(y_ready, t + 1)
                if not first(t, 4):
                    act.wait_ge(out_ready, t - 3)
                act.activation(y_sb[:, k % 4, H:D], y_ps[:, k % 2, 1, 0:H], ACT.Copy).then_inc(y_right_ok, 1)
                act.activation(y_sb[:, k % 4, 0:H], y_ps[:, k % 2, 0, 0:H], ACT.Copy).then_inc(y_left_ok, 1)

            def variance(t, k):
                act.wait_ge(nmean_ready, t + 1)
                if not first(t, 1):
                    act.wait_ge(var1_ready, t)
                act.activation(squares[:, :], x1[:, k % 2, :], ACT.Square, bias=x1_nmean[:, k % 2:k % 2 + 1],
                               scale=D ** -0.5, accum_out=x1_var[:, k % 4:k % 4 + 1]).then_inc(var1_ready, 1)

            def step(t, k):
                if real(t - 1):
                    act.wait_ge(pt_ready, t)
                    if not first(t, 2):
                        act.wait_ge(y_ready, t - 1)
                    act.activation(pT[:, :, :], p_transposed((k - 1) % 2), ACT.Copy).then_inc(pT_ready, 1)
                if tail(t - 1):
                    evacuate(t - 2, k - 2)
                    variance(t - 2, k - 2)
                if real(t + 1):
                    j = (k + 1) % 2
                    act.wait_ge(xt_ready, t + 2)
                    if not first(t, 1):
                        act.wait_ge(x_done, t)
                    act.activation(xT[:, j, 0, :, :], xt_ps[:, j, :, :], ACT.Copy).then_inc(xh_ready, 1)
                if k == SWITCH and not isinstance(t, int):
                    ctx_columns((t - k) // TB + 1)
                if real(t - 1) and not tail(t):
                    evacuate(t - 1, k - 1)
                if real(t):
                    j = k % 2
                    act.wait_ge(nmax_ready, t + 1)
                    act.activation(expd[:, j, :], scores(j), ACT.Exp, bias=neg_max[:, j:j + 1],
                                   scale=rstd[:, k % 4:k % 4 + 1], accum_out=e_sum[:, j:j + 1]).then_inc(exp_done, 1)
                if real(t - 1) and not tail(t):
                    variance(t - 1, k - 1)
                if k == STATS and not isinstance(t, int):
                    ctx_rows_hi((t - k) // TB + 1)
                if k == TAKE and not isinstance(t, int):
                    ctx_product_hi((t - k) // TB + 1)

            act.wait_ge(ld_gates, 16)
            act.activation(tg[:, :], b_row[:, D:D + 2], ACT.Tanh).then_inc(tg_ok, 1)
            act.wait_ge(ld_w[1], 16)
            for i in range(2):
                act.activation(w_cent[:, 2 + i, :], w_rows[:, 2 + i, :], ACT.Copy, scale=-1.0 / D,
                               accum_out=w_nmean[:, i:i + 1]).then_inc(w_nmean_ok, 1)
            act.wait_ge(low_mm, 2)
            act.activation(up_st[:, :], c_ps[0:LR, :], ACT.Copy).then_inc(up_hi_ok, 1)
            for i in range(2):
                act.wait_ge(w_nmean_ok, i + 1)
                act.activation(w_cent[:, 2 + i, :], w_rows[:, 2 + i, :], ACT.Identity, bias=w_nmean[:, i:i + 1])\
                    .then_inc(w_centred[1], 1)
            step(-1, -1)
            act.wait_ge(tg_ok, 1)
            for c in range(KC):
                act.wait_ge(w_tr, c + 1)
                act.activation(wc[:, c, 0, 0:D], w_bank(c), ACT.Copy, scale=tg[:, 1:2]).then_inc(w_hi_ok, 1)
                if c == 0:
                    prep(0, TURN)
            ctx_rows_hi(0)
            ctx_columns(0)
            ctx_product_hi(0)
            act.wait_ge(ld_b, 16)
            act.activation(bias_g[:, :], b_row[:, 0:D], ACT.Copy, scale=tg[:, 1:2]).then_inc(biasg_ok, 1)
            all_tiles(act, step, prep)

        @block.tensor
        def _(pe):
            pe.wait_ge(ld_in, 16)
            pe.matmul(a_ps[0:LR, :], low_in_sb[:, 0:LR], low_in_sb[:, LR:LR + D], start=True, stop=True)\
                .then_inc(low_mm, 1)
            pe.wait_ge(ld_out, 16)
            pe.matmul(c_ps[0:LR, :], low_out_sb[:, 0:LR], low_out_sb[:, LR:LR + D], start=True, stop=True)\
                .then_inc(low_mm, 1)

            def prep(n, k):
                if k == TURN:
                    pe.wait_ge(c_centred, n + 1)
                    if isinstance(n, int):
                        pe.wait_ge(up_ok, 1)
                    else:
                        pe.wait_ge(v_lo_ok, 2 * n)
                    for c in range(KC):
                        mm = pe.transpose(ct_ps[:, c, :], c_cent[:, c * P:(c + 1) * P], ident[0:V, 0:V])
                    mm.then_inc(c_tr, 1)
                if k == PRODUCT:
                    pe.wait_ge(ct_hi_ok, n + 1)
                    if not isinstance(n, int):
                        pe.wait_ge(ct_lo_ok, n + 1)
                    m = 0
                    for c in range(KC):
                        for lhs, rhs in ((0, 0), (0, 1), (1, 0)):
                            if isinstance(n, int) and lhs == 1 and c == 0:
                                pe.wait_ge(ct_lo_ok, 1)
                            if isinstance(n, int) and lhs == 0:
                                pe.wait_ge(w_lo_ok if rhs else w_hi_ok, c + 1)
                            mm = pe.matmul(cw_ps(n), ct[:, lhs, c, :], wc[:, c, rhs, 0:D],
                                           start=(m == 0), stop=(m == 3 * KC - 1))
                            m += 1
                    mm.then_inc(cw_mm, 1)

            def x_transposes(t, k):
                x_landed(pe, t, k)
                if not first(t, 2):
                    pe.wait_ge(xl_ready, t - 1)
                for c in range(KC):
                    mm = pe.transpose(xt_ps[:, k % 2, c, :], x_sb[:, k % XRING, c * P:(c + 1) * P], ident[:, :])
                mm.then_inc(xt_ready, 1)

            def x_product(t, k, h, chunks):
                n = H if h == 0 else H + VP
                for c in chunks:
                    for part, w in ((0, 0), (0, 1), (1, 0)):
                        mm = pe.matmul(y_ps[:, k % 2, h, 0:n], xT[:, k % 2, part, c, :], wc[:, c, w, h * H:h * H + n],
                                       start=(c == 0 and part == 0 and w == 0),
                                       stop=(c == KC - 1 and part == 1), skip_group_check=True)
                if c == KC - 1:
                    mm.then_inc(s_ready if h == 1 else x_done, 1)

            def p_transposes(t, k):
                pe.wait_ge(p_ready, t + 1)
                for s in range(2):
                    mm = pe.matmul(p_transposed(k % 2)[:, s, :], p_ext[:, s * K2:(s + 1) * K2], ident[:, :],
                                   is_transpose=True, start=False, stop=True, skip_group_check=True)
                mm.then_inc(pt_ready, 1)

            def p_product(t, k):
                pe.wait_ge(pT_ready, t + 1)
                pair = k % TB // HB
                if k % HB == 0:
                    pe.wait_ge(stacked[pair], 64 * (t // TB + 1) if isinstance(t, int) else 4 * (t - k % TB + TB))
                if not first(t, 1):
                    pe.wait_ge(x1_ready, t)
                for s in range(2):
                    mm = pe.matmul(a_ps[:, :], pT[:, s, :], stacks[:, pair, s, 0:D], start=(s == 0), stop=(s == 1))
                mm.then_inc(a_ready, 1)
                for h in (1, 0):
                    for s in range(2):
                        mm = pe.matmul(y_ps[:, k % 2, h, 0:H], pT[:, s, :], stacks[:, pair, s, D + h * H:D + (h + 1) * H],
                                       start=False, stop=(s == 1), skip_group_check=True)
                mm.then_inc(y_ready, 1)

            def step(t, k):
                if real(t):
                    pe.wait_ge(xl_ready, t + 1)
                    if not first(t, 2):
                        pe.wait_ge(y_right_ok, t - 1)
                    if k % TB == 0:
                        pe.wait_ge(c_cols, 2 * (t // TB) + 2 if isinstance(t, int) else (t + TB) // (TB // 2))
                    x_product(t, k, 1, range(KC - 1))
                if real(t - 1):
                    p_transposes(t - 1, k - 1)
                if real(t + 1):
                    x_transposes(t + 1, k + 1)
                if real(t):
                    x_product(t, k, 1, range(KC - 1, KC))
                if real(t - 1) and not tail(t):
                    p_product(t - 1, k - 1)
                if real(t):
                    if not first(t, 2):
                        pe.wait_ge(y_left_ok, t - 1)
                    x_product(t, k, 0, range(KC))
                if tail(t):
                    p_product(t - 1, k - 1)

            def w_transposes(half):
                for i in range(2):
                    pe.wait_ge(w_centred[half], i + 1)
                    o = 2 * half + i
                    for c in range(KC):
                        pe.matmul(w_bank(c)[:, o * P:(o + 1) * P], w_cent[:, o, c * P:(c + 1) * P], ident[:, :],
                                  is_transpose=True, start=(o == 0), stop=False, skip_group_check=True)

            pe.wait_ge(ident_ok, 4)
            w_transposes(0)
            step(-1, -1)
            w_transposes(1)
            pe.wait_ge(dn_ok, 1)
            pe.wait_ge(up_ok, 1)
            for c in range(KC):
                pe.matmul(w_bank(c), dn_st[:, c * P:(c + 1) * P], up_st[:, :], start=False, stop=True,
                          skip_group_check=True).then_inc(w_tr, 1)
            prep(0, TURN)
            prep(0, PRODUCT)
            all_tiles(pe, step, prep)

        @block.vector
        def _(dve):
            dve.memset(p_ext[:, :], 0.0).then_inc(hi_own, 1)

            def ctx_rows_lo(n):
                dve.wait_ge(c_own, 2 * n + 1)
                dve.wait_ge(v_hi_ok, 2 * n + 1)
                dve.scalar_tensor_tensor(out=v_lo[:, 0:D], in0=c_rows[:, :], scalar=tg[0:V, 0:1],
                                         in1=v_hi[:, 0:D].bitcast(F32), op0=ALU.mult, op1=ALU.subtract)\
                    .then_inc(v_lo_ok, 1)

            def ctx_mean(n):
                dve.bn_aggr(c_mv[:, :], c_bn[:, :]).then_inc(c_own, 1)

            def prep(n, k):
                if k == STATS:
                    dve.wait_ge(ld_ctx, 16 * n + 16)
                    dve.bn_stats(c_bn[:, :], c_rows[:, :]).then_inc(c_own, 1)
                if k == ROWS:
                    ctx_rows_lo(n)
                    ctx_mean(n)
                if k == CENTRE:
                    dve.wait_ge(c_own, 2 * n + 2)
                    dve.tensor_scalar(c_cent[:, :], c_rows[:, :], c_mv[:, 0:1], None, ALU.subtract)\
                        .then_inc(c_centred, 1)
                if k == TURN:
                    dve.wait_ge(ct_hi_ok, n + 1)
                    dve.tensor_tensor(ct[:, 1, :, :], ct_ps, ct[:, 0, :, :].bitcast(F32), ALU.subtract)\
                        .then_inc(ct_lo_ok, 1)
                if k == TAKE:
                    dve.wait_ge(v_hi_ok, 2 * n + 2)
                    dve.scalar_tensor_tensor(out=v_lo[:, D:2 * D], in0=cw_ps(n), scalar=tg[0:V, 0:1],
                                             in1=v_hi[:, D:2 * D].bitcast(F32), op0=ALU.mult, op1=ALU.subtract)\
                        .then_inc(v_lo_ok, 1)

            p_pair = p_ext[:, :].rearrange("p (a v) -> p a v", a=2)[:, :, 0:V].bitcast(F32R)

            def x_transposed_lo(t, k):
                dve.wait_ge(xh_ready, t + 1)
                dve.tensor_tensor(xT[:, k % 2, 1, :, :], xt_ps[:, k % 2, :, :], xT[:, k % 2, 0, :, :].bitcast(F32),
                                  ALU.subtract).then_inc(xl_ready, 1)

            def row_stats(t, k):
                x_landed(dve, t, k)
                dve.bn_stats(bn[:, k % 2, :], x_sb[:, k % XRING, :]).then_inc(bn_ok, 1)

            def row_mean_var(t, k):
                dve.bn_aggr(mv[:, k % 4, :], bn[:, k % 2, :]).then_inc(mv_ready, 1)

            def x1_rows(t, k):
                j = k % 2
                dve.wait_ge(a_ready, t + 1)
                if not first(t, 2):
                    dve.wait_ge(var1_ready, t - 1)
                    dve.wait_ge(x1b_ready, t - 1)
                dve.scalar_tensor_tensor(out=x1[:, j, :], in0=a_ps[:, :], scalar=1.0, in1=x_sb[:, k % XRING, :],
                                         op0=ALU.mult, op1=ALU.add, accum_out=x1_sum[:, j:j + 1])\
                    .then_inc(x1_ready, 1)
                dve.wait_ge(x1_ready, t + 1)
                dve.tensor_scalar(x1_nmean[:, j:j + 1], x1_sum[:, j:j + 1], -D ** -1.5, None, ALU.mult)\
                    .then_inc(nmean_ready, 1)

            def probabilities(t, k):
                j = k % 2
                dve.wait_ge(exp_done, t + 1)
                dve.reciprocal(e_inv[:, j:j + 1], e_sum[:, j:j + 1]).then_inc(inv_own, 1)
                dve.wait_ge(inv_own, t + 1)
                if first(t, 1):
                    dve.wait_ge(hi_own, 1)
                else:
                    dve.wait_ge(pt_ready, t)
                dve.tensor_scalar(p_pair, expd[:, j:j + 1, :].to_broadcast([P, 2, V]), e_inv[:, j:j + 1], None,
                                  ALU.mult).then_inc(hi_own, 1)
                dve.wait_ge(hi_own, t + 2)
                dve.scalar_tensor_tensor(out=p_ext[:, V:2 * V].bitcast(F32R), in0=expd[:, j, :],
                                         scalar=e_inv[:, j:j + 1], in1=p_ext[:, 0:V],
                                         op0=ALU.mult, op1=ALU.subtract).then_inc(p_ready, 1)

            def output(t, k):
                q = k % 4
                dve.wait_ge(y_left_ok, t + 1)
                dve.wait_ge(rstd1_ready, t + 1)
                if isinstance(t, int) and t == T - 1:
                    dve.wait_ge(last_x1b_ready, 1)
                else:
                    dve.wait_ge(x1b_ready, t + 1)
                if not first(t, ORING):
                    dve.wait_ge(st_o[q // UNIT], 16 * unit_turn(t, k, ORING))
                dve.scalar_tensor_tensor(out=o_sb[:, q, :], in0=y_sb[:, q, :], scalar=rstd1[:, q:q + 1],
                                         in1=x1_bias[:, q, :], op0=ALU.mult, op1=ALU.add).then_inc(out_ready, 1)

            def step(t, k):
                j, i = k % 2, (k - 1) % 2
                if real(t):
                    dve.wait_ge(s_ready, t + 1)
                    dve.reduce_max(s_max[:, j:j + 1], scores(j), AX.X).then_inc(max_own, 1)
                    dve.wait_ge(max_own, t + 1)
                    dve.wait_ge(rstd_ready, t + 1)
                    dve.tensor_scalar(neg_max[:, j:j + 1], s_max[:, j:j + 1], rstd[:, k % 4:k % 4 + 1], -1.0,
                                      ALU.mult, ALU.mult).then_inc(nmax_ready, 1)
                if real(t + 1):
                    x_transposed_lo(t + 1, k + 1)
                if real(t - 1) and not tail(t):
                    x1_rows(t - 1, k - 1)
                if real(t):
                    probabilities(t, k)
                if tail(t):
                    x1_rows(t - 1, k - 1)
                if real(t + 2):
                    row_stats(t + 2, k + 2)
                if real(t + 2):
                    dve.wait_ge(bn_ok, t + 3)
                if real(t - 2):
                    if not real(t):
                        dve.wait_ge(out_ready, T - 4)
                        dve.tensor_tensor(x1_bias[:, (k - 1) % 4, :], x1[:, i, :], bias_g[:, :], ALU.add)\
                            .then_inc(last_x1b_ready, 1)
                    output(t - 2, k - 2)
                if real(t + 2):
                    row_mean_var(t + 2, k + 2)

            dve.wait_ge(ld_w[0], 16)
            for c in range(2):
                dve.bn_stats(w_bn[:, c, :], w_rows[:, c, :]).then_inc(w_own, 1)
            for c in range(2):
                dve.wait_ge(w_own, c + 1)
                dve.bn_aggr(w_mv[:, c, :], w_bn[:, c, :]).then_inc(w_own, 1)
            for c in range(2):
                dve.wait_ge(w_own, 2 + c + 1)
                dve.tensor_scalar(w_cent[:, c, :], w_rows[:, c, :], w_mv[:, c, 0:1], None, ALU.subtract)\
                    .then_inc(w_centred[0], 1)
            dve.wait_ge(low_mm, 1)
            dve.bn_stats(dn_bn[:, :], a_ps[0:LR, :]).then_inc(dn_own, 1)
            dve.wait_ge(dn_own, 1)
            dve.bn_aggr(dn_mv[:, :], dn_bn[:, :]).then_inc(dn_own, 1)
            dve.wait_ge(dn_own, 2)
            dve.tensor_scalar(dn_st[:, :], a_ps[0:LR, :], dn_mv[:, 0:1], None, ALU.subtract).then_inc(dn_own, 1)
            dve.wait_ge(dn_own, 3)
            dve.scalar_tensor_tensor(out=dn_st[2 * LQ:LR, :], in0=a_ps[2 * LQ:LR, :], scalar=dn_mv[2 * LQ:LR, 0:1],
                                     in1=dn_st[2 * LQ:LR, :].bitcast(F32), op0=ALU.subtract, op1=ALU.subtract)\
                .then_inc(dn_ok, 1)
            dve.wait_ge(up_hi_ok, 1)
            dve.tensor_tensor(up_st[LQ:2 * LQ, :], c_ps[LQ:2 * LQ, :], up_st[LQ:2 * LQ, :].bitcast(F32),
                              ALU.subtract).then_inc(up_ok, 1)
            prep(0, STATS)
            dve.wait_ge(c_own, 1)
            ctx_mean(0)
            prep(0, CENTRE)
            x_transposed_lo(0, 0)
            dve.wait_ge(tg_ok, 1)
            for c in range(KC):
                dve.wait_ge(w_hi_ok, c + 1)
                dve.scalar_tensor_tensor(out=wc[:, c, 1, 0:D], in0=w_bank(c), scalar=tg[:, 1:2],
                                         in1=wc[:, c, 0, 0:D].bitcast(F32), op0=ALU.mult, op1=ALU.subtract)\
                    .then_inc(w_lo_ok, 1)
                if c == 0:
                    prep(0, TURN)
            ctx_rows_lo(0)
            row_stats(0, 0)
            dve.wait_ge(bn_ok, 1)
            row_mean_var(0, 0)
            prep(0, TAKE)
            row_stats(1, 1)
            dve.wait_ge(bn_ok, 2)
            row_mean_var(1, 1)
            all_tiles(dve, step, prep)
            output(T - 1, TB - 1)


def kernel(x, ctx_1024, g_xattn, g_ffn, L0_ffn_W, L0_ffn_b, L0_ffn_lora_down, L0_ffn_lora_up,
           L0_ffn_down_aux, L0_ffn_up_aux):
    import numpy as np
    import concourse.bacc as bacc
    from concourse.bass_utils import run_bass_kernel_spmd

    nc = bacc.Bacc("TRN2", target_bir_lowering=False, num_devices=1)
    def thrice(a):
        wide = np.zeros((a.shape[0], 64 + a.shape[1]), a.dtype)
        for q in range(3):
            wide[:, 32 * q:32 * q + a.shape[1]] = a
        return wide

    ins = {
        "x": x, "ctx": ctx_1024, "w": L0_ffn_W,
        "b_gates": np.concatenate([L0_ffn_b, g_xattn, g_ffn]),
        "low_in": np.concatenate([thrice(np.transpose(L0_ffn_lora_down)), L0_ffn_down_aux], axis=1),
        "low_out": np.concatenate([thrice(L0_ffn_lora_up), np.transpose(L0_ffn_up_aux)], axis=1),
    }
    arrays, args = {}, []
    for name, a in ins.items():
        arrays[f"in_{name}"] = np.ascontiguousarray(a)
        args.append(nc.dram_tensor(f"in_{name}", arrays[f"in_{name}"].shape, mybir.dt.from_np(arrays[f"in_{name}"].dtype),
                                   kind="ExternalInput").ap())
    out = nc.dram_tensor("out", x.shape, F32, kind="ExternalOutput").ap()
    build_kernel(nc, *args, out)
    r = run_bass_kernel_spmd(nc, [arrays], core_ids=[0])
    return r.results[0]["out"]
```
